# Optimizing a Trainium2 kernel written in Bass

```python
import numpy as np
import jax
import jax.numpy as jnp

def _softmax(x, axis=-1):
    return jax.nn.softmax(x, axis=axis)

def _gelu(x):
    return jax.nn.gelu(x, approximate=True)

def _silu(x):
    return jax.nn.silu(x)

def _sigmoid(x):
    return jax.nn.sigmoid(x)

def _layernorm(x, axis=-1, eps=1e-05):
    m = jnp.mean(x, axis=axis, keepdims=True)
    v = jnp.var(x, axis=axis, keepdims=True)
    return (x - m) / jnp.sqrt(v + eps)

def _scatter_add(tgt, idx, src, axis=0):
    return tgt.at[idx].add(src)

def _segment_sum(src, seg, n):
    return jax.ops.segment_sum(src, seg, n)
kernel_name = 'mk_perceiver_d2_seqx_r4_c8f04e'

def setup_inputs(seed: int=0):
    np.random.seed(seed)
    _w = jnp.asarray

    def _rec_inputs():
        import jax
        import jax.numpy as jnp
        _rk = jax.random.key(seed)
        x = 7.22e-05 + 1 * jax.random.normal(jax.random.fold_in(_rk, 1), (2, 256, 256), jnp.float32)
        _lenS = 256 - jax.random.randint(jax.random.fold_in(_rk, 7), (2,), 0, max(1, 256 // 4) + 1, jnp.int32)
        _lenS2 = 4096 - jax.random.randint(jax.random.fold_in(_rk, 8), (2,), 0, max(1, 4096 // 4) + 1, jnp.int32)
        _ctx_1024P = jax.random.normal(jax.random.fold_in(_rk, 11), (2, 16, 256), jnp.float32)
        _ctx_1024c = jax.random.dirichlet(jax.random.fold_in(_rk, 511), 0.3 * jnp.ones((16,), jnp.float32), (2, 4096))
        _ctx_1024t = jnp.einsum('bsk,bkd->bsd', _ctx_1024c, _ctx_1024P)
        _ctx_1024t = _ctx_1024t * jax.lax.rsqrt(jnp.mean(jnp.square(_ctx_1024t)) + 1e-12) * 0.953939
        ctx_1024 = -4.77421e-07 + 0.031248 * (_ctx_1024t + 0.3 * jax.random.normal(jax.random.fold_in(_rk, 611), (2, 4096, 256), jnp.float32))
        _validS = jnp.arange(256)[None, :] < _lenS[:, None]
        _validS2 = jnp.arange(4096)[None, :] < _lenS2[:, None]
        _causal = jnp.tril(jnp.ones((256, 256), dtype=bool))
        mask_1x1xSxS2_ik0 = jnp.where(jnp.broadcast_to(_validS2[0:1, None, None, :], (1, 1, 256, 4096)), 0, 1).astype(jnp.int32)
        return (x, ctx_1024, mask_1x1xSxS2_ik0)
    x, ctx_1024, mask_1x1xSxS2_ik0 = _rec_inputs()

    def _L0_xattn_setup():
        import jax, jax.numpy as jnp
        import numpy as np
        E, T, H, F = (8, 256, 256, 1024)
        key = jax.random.key(seed)
        k1, k2, k3 = jax.random.split(key, 3)
        x = jax.random.normal(k1, (E, T, H), dtype=jnp.float32)
        w1 = jax.random.normal(k2, (E, F, H), dtype=jnp.float32) * (1.0 / np.sqrt(H))
        w2 = jax.random.normal(k3, (E, F, H), dtype=jnp.float32) * (1.0 / np.sqrt(F))
        return {'x': x, 'w1': w1, 'w2': w2}
    _L0_xattn_all = _L0_xattn_setup()
    _L0_xattn_in = {k: v for k, v in _L0_xattn_all.items() if k in ()}
    del _L0_xattn_all

    def _L0_attn_setup():
        import jax, jax.numpy as jnp
        import numpy as np
        import math
        D_MODEL, N_HEADS, D_K, D_C, D_HR = (256, 8, 128, 32, 32)
        B, S = (4, 512)
        key = jax.random.key(seed)
        ks = jax.random.split(key, 17)

        def lin(k, fan_in, fan_out):
            lim = 1.0 / math.sqrt(fan_in)
            kw, kb = jax.random.split(k)
            W = jax.random.uniform(kw, (fan_in, fan_out), jnp.float32, -lim, lim)
            b = jax.random.uniform(kb, (fan_out,), jnp.float32, -lim, lim)
            return (W, b)
        W_DQ, b_DQ = lin(ks[0], D_MODEL, D_C)
        W_UQ, b_UQ = lin(ks[1], D_C, N_HEADS * D_K)
        W_DKV, b_DKV = lin(ks[2], D_MODEL, D_C)
        W_UK, b_UK = lin(ks[3], D_C, N_HEADS * D_K)
        W_UV, b_UV = lin(ks[4], D_C, N_HEADS * D_K)
        W_QR, b_QR = lin(ks[5], D_C, N_HEADS * D_HR)
        W_KR, b_KR = lin(ks[6], D_MODEL, D_HR)
        W_O, b_O = lin(ks[7], N_HEADS * D_K, D_MODEL)
        h_t = jax.random.normal(ks[8], (B, S, D_MODEL), jnp.float32)
        return {'h_t': h_t, 'W_DQ': W_DQ, 'b_DQ': b_DQ, 'W_UQ': W_UQ, 'b_UQ': b_UQ, 'W_DKV': W_DKV, 'b_DKV': b_DKV, 'W_UK': W_UK, 'b_UK': b_UK, 'W_UV': W_UV, 'b_UV': b_UV, 'W_QR': W_QR, 'b_QR': b_QR, 'W_KR': W_KR, 'b_KR': b_KR, 'W_O': W_O, 'b_O': b_O}
    _L0_attn_all = _L0_attn_setup()
    _L0_attn_in = {k: v for k, v in _L0_attn_all.items() if k in ('W_DQ', 'b_DQ', 'W_UQ', 'b_UQ', 'W_DKV', 'b_DKV', 'W_UK', 'b_UK', 'W_UV', 'b_UV', 'W_QR', 'b_QR', 'W_KR', 'b_KR', 'W_O', 'b_O')}
    del _L0_attn_all

    def _L0_ffn_setup():
        import jax, jax.numpy as jnp
        import numpy as np
        H = 256
        D = 688
        E = 8
        TOP_K = 2

        def _moe_ffn(x, gate_w, we_gate, we_up, we_down, sw_gate, sw_up, sw_down):
            B, S, h = x.shape
            xt = x.reshape(-1, h)
            T = xt.shape[0]
            logits = xt @ gate_w.T
            probs = jax.nn.softmax(logits, axis=-1)
            topk_w, topk_idx = jax.lax.top_k(probs, TOP_K)
            topk_w = topk_w / (jnp.sum(topk_w, axis=-1, keepdims=True) + 1e-20)
            cw = jnp.zeros((T, E), dtype=xt.dtype).at[jnp.arange(T)[:, None], topk_idx].add(topk_w)
            g = jnp.einsum('th,ehd->etd', xt, we_gate)
            u = jnp.einsum('th,ehd->etd', xt, we_up)
            hidden = jax.nn.silu(g) * u
            eo = jnp.einsum('etd,edh->eth', hidden, we_down)
            y = jnp.einsum('te,eth->th', cw, eo)
            y = y + jax.nn.silu(xt @ sw_gate) * (xt @ sw_up) @ sw_down
            return y.reshape(B, S, h)
        key = jax.random.key(seed)
        ks = jax.random.split(key, 8)
        s = 0.02
        return {'x': jax.random.normal(ks[0], (2, 512, H), dtype=jnp.float32), 'gate_w': jax.random.normal(ks[1], (E, H), dtype=jnp.float32) * s, 'we_gate': jax.random.normal(ks[2], (E, H, D), dtype=jnp.float32) * s, 'we_up': jax.random.normal(ks[3], (E, H, D), dtype=jnp.float32) * s, 'we_down': jax.random.normal(ks[4], (E, D, H), dtype=jnp.float32) * s, 'sw_gate': jax.random.normal(ks[5], (H, D), dtype=jnp.float32) * s, 'sw_up': jax.random.normal(ks[6], (H, D), dtype=jnp.float32) * s, 'sw_down': jax.random.normal(ks[7], (D, H), dtype=jnp.float32) * s}
    _L0_ffn_all = _L0_ffn_setup()
    _L0_ffn_in = {k: v for k, v in _L0_ffn_all.items() if k in ('gate_w', 'we_gate', 'we_up', 'we_down', 'sw_gate', 'sw_up', 'sw_down')}
    del _L0_ffn_all

    def _L1_xattn_setup():
        import jax, jax.numpy as jnp
        import numpy as np
        import math
        EMBED = 256
        HEADS = 16
        HEAD_DIM = EMBED // HEADS
        WINDOW = 128
        B, S = (2, 512)
        key = jax.random.key(seed)
        k1, k2, k3, k4 = jax.random.split(key, 4)
        values = jax.random.normal(k1, (B, S, EMBED), dtype=jnp.float32)
        keys = jax.random.normal(k2, (B, S, EMBED), dtype=jnp.float32)
        queries = jax.random.normal(k3, (B, S, EMBED), dtype=jnp.float32)
        idx = jnp.arange(S)
        band = (jnp.abs(idx[:, None] - idx[None, :]) <= WINDOW // 2).astype(jnp.int32)
        mask = band[None, None, :, :]
        w_out = jax.random.normal(k4, (EMBED, EMBED), dtype=jnp.float32) * (1.0 / math.sqrt(EMBED))
        b_out = jnp.zeros((EMBED,), dtype=jnp.float32)
        return {'values': values, 'keys': keys, 'queries': queries, 'mask': mask, 'w_out': w_out, 'b_out': b_out}
    _L1_xattn_all = _L1_xattn_setup()
    _L1_xattn_in = {k: v for k, v in _L1_xattn_all.items() if k in ('w_out', 'b_out')}
    del _L1_xattn_all

    def _L1_attn_setup():
        import jax, jax.numpy as jnp
        import numpy as np
        EPS = 1e-08

        def unit_projection(x):
            f = jnp.fft.fft(x)
            f = f / (jnp.abs(f) + EPS)
            return jnp.fft.ifft(f).real

        def bind(a, b):
            return jnp.fft.ifft(jnp.fft.fft(a) * jnp.fft.fft(b)).real

        def unbind(s, a):
            return jnp.fft.ifft(jnp.fft.fft(s) * jnp.conj(jnp.fft.fft(a))).real
        key = jax.random.key(seed)
        B, S, D = (4, 1024, 256)
        ks = jax.random.split(key, 7)
        scale = 1.0 / np.sqrt(D)
        x = jax.random.normal(ks[0], (B, S, D), dtype=jnp.float32)
        Wq = jax.random.uniform(ks[1], (D, D), jnp.float32, -scale, scale)
        bq = jax.random.uniform(ks[2], (D,), jnp.float32, -scale, scale)
        Wk = jax.random.uniform(ks[3], (D, D), jnp.float32, -scale, scale)
        bk = jax.random.uniform(ks[4], (D,), jnp.float32, -scale, scale)
        Wv = jax.random.uniform(ks[5], (D, D), jnp.float32, -scale, scale)
        bv = jax.random.uniform(ks[6], (D,), jnp.float32, -scale, scale)
        return {'x': x, 'Wq': Wq, 'bq': bq, 'Wk': Wk, 'bk': bk, 'Wv': Wv, 'bv': bv}
    _L1_attn_all = _L1_attn_setup()
    _L1_attn_in = {k: v for k, v in _L1_attn_all.items() if k in ('Wq', 'bq', 'Wk', 'bk', 'Wv', 'bv')}
    del _L1_attn_all

    def _L1_ffn_setup():
        import jax, jax.numpy as jnp
        import numpy as np
        HIDDEN = 256
        HEAD_DIM = 64
        N_EXPERTS = 16
        MIN_EXPERTS = 2
        B, T = (4, 512)

        def _normalize(x, axis):
            n = jnp.sqrt(jnp.sum(x * x, axis=axis, keepdims=True))
            return x / jnp.maximum(n, 1e-12)

        def _ste(x):
            hard = jax.lax.stop_gradient((x > 0).astype(x.dtype))
            return hard + x - jax.lax.stop_gradient(x)

        def _gating(hidden_states, sim_matrix, gates):
            b, t, c = hidden_states.shape
            flat = hidden_states.reshape(b * t, c)
            logits = _normalize(flat, -1) @ _normalize(sim_matrix, 0) - jax.nn.sigmoid(gates)
            gated = jax.nn.relu(logits)
            mask = _ste(gated)
            inactive = jnp.sum(mask, axis=1) == 0
            _, fb_idx = jax.lax.top_k(logits, MIN_EXPERTS)
            fb = jnp.zeros_like(mask).at[jnp.arange(b * t)[:, None], fb_idx].set(1.0)
            fb_applied = inactive[:, None] & (fb > 0)
            mask = jnp.where(fb_applied, 1.0, mask)
            masked_logits = jnp.where(mask > 0, gated, -jnp.inf)
            return jax.nn.softmax(masked_logits, axis=-1).reshape(b, t, -1)
        key = jax.random.key(seed)
        ks = jax.random.split(key, 6)
        xav_qkv = float(np.sqrt(6.0 / (HIDDEN + HEAD_DIM)))
        return {'hidden_states': jax.random.normal(ks[0], (B, T, HIDDEN), dtype=jnp.float32), 'sim_matrix': jax.random.normal(ks[1], (HIDDEN, N_EXPERTS), dtype=jnp.float32), 'gates': jnp.zeros((N_EXPERTS,), dtype=jnp.float32), 'q_proj': jax.random.uniform(ks[2], (N_EXPERTS, HIDDEN, HEAD_DIM), jnp.float32, -xav_qkv, xav_qkv), 'k_proj': jax.random.uniform(ks[3], (N_EXPERTS, HIDDEN, HEAD_DIM), jnp.float32, -xav_qkv, xav_qkv), 'v_proj': jax.random.uniform(ks[4], (N_EXPERTS, HIDDEN, HEAD_DIM), jnp.float32, -xav_qkv, xav_qkv), 'o_proj': jax.random.uniform(ks[5], (N_EXPERTS, HEAD_DIM, HIDDEN), jnp.float32, -xav_qkv, xav_qkv)}
    _L1_ffn_all = _L1_ffn_setup()
    _L1_ffn_in = {k: v for k, v in _L1_ffn_all.items() if k in ('sim_matrix', 'gates', 'q_proj', 'k_proj', 'v_proj', 'o_proj')}
    del _L1_ffn_all
    return {'x': x, 'ctx_1024': ctx_1024, 'mask_1x1xSxS2_ik0': mask_1x1xSxS2_ik0, 'L0_attn_W_DQ': _L0_attn_in['W_DQ'], 'L0_attn_b_DQ': _L0_attn_in['b_DQ'], 'L0_attn_W_UQ': _L0_attn_in['W_UQ'], 'L0_attn_b_UQ': _L0_attn_in['b_UQ'], 'L0_attn_W_DKV': _L0_attn_in['W_DKV'], 'L0_attn_b_DKV': _L0_attn_in['b_DKV'], 'L0_attn_W_UK': _L0_attn_in['W_UK'], 'L0_attn_b_UK': _L0_attn_in['b_UK'], 'L0_attn_W_UV': _L0_attn_in['W_UV'], 'L0_attn_b_UV': _L0_attn_in['b_UV'], 'L0_attn_W_QR': _L0_attn_in['W_QR'], 'L0_attn_b_QR': _L0_attn_in['b_QR'], 'L0_attn_W_KR': _L0_attn_in['W_KR'], 'L0_attn_b_KR': _L0_attn_in['b_KR'], 'L0_attn_W_O': _L0_attn_in['W_O'], 'L0_attn_b_O': _L0_attn_in['b_O'], 'L0_ffn_gate_w': _L0_ffn_in['gate_w'], 'L0_ffn_we_gate': _L0_ffn_in['we_gate'], 'L0_ffn_we_up': _L0_ffn_in['we_up'], 'L0_ffn_we_down': _L0_ffn_in['we_down'], 'L0_ffn_sw_gate': _L0_ffn_in['sw_gate'], 'L0_ffn_sw_up': _L0_ffn_in['sw_up'], 'L0_ffn_sw_down': _L0_ffn_in['sw_down'], 'L1_xattn_w_out': _L1_xattn_in['w_out'], 'L1_xattn_b_out': _L1_xattn_in['b_out'], 'L1_attn_Wq': _L1_attn_in['Wq'], 'L1_attn_bq': _L1_attn_in['bq'], 'L1_attn_Wk': _L1_attn_in['Wk'], 'L1_attn_bk': _L1_attn_in['bk'], 'L1_attn_Wv': _L1_attn_in['Wv'], 'L1_attn_bv': _L1_attn_in['bv'], 'L1_ffn_sim_matrix': _L1_ffn_in['sim_matrix'], 'L1_ffn_gates': _L1_ffn_in['gates'], 'L1_ffn_q_proj': _L1_ffn_in['q_proj'], 'L1_ffn_k_proj': _L1_ffn_in['k_proj'], 'L1_ffn_v_proj': _L1_ffn_in['v_proj'], 'L1_ffn_o_proj': _L1_ffn_in['o_proj']}

def reference(x, ctx_1024, mask_1x1xSxS2_ik0, L0_attn_W_DQ, L0_attn_b_DQ, L0_attn_W_UQ, L0_attn_b_UQ, L0_attn_W_DKV, L0_attn_b_DKV, L0_attn_W_UK, L0_attn_b_UK, L0_attn_W_UV, L0_attn_b_UV, L0_attn_W_QR, L0_attn_b_QR, L0_attn_W_KR, L0_attn_b_KR, L0_attn_W_O, L0_attn_b_O, L0_ffn_gate_w, L0_ffn_we_gate, L0_ffn_we_up, L0_ffn_we_down, L0_ffn_sw_gate, L0_ffn_sw_up, L0_ffn_sw_down, L1_xattn_w_out, L1_xattn_b_out, L1_attn_Wq, L1_attn_bq, L1_attn_Wk, L1_attn_bk, L1_attn_Wv, L1_attn_bv, L1_ffn_sim_matrix, L1_ffn_gates, L1_ffn_q_proj, L1_ffn_k_proj, L1_ffn_v_proj, L1_ffn_o_proj):
    import jax
    import jax.numpy as jnp

    def _L0_xattn_ref(x, w1, w2):
        import jax, jax.numpy as jnp
        import numpy as np
        E, T, H, F = (8, 256, 256, 1024)
        h = jnp.einsum('eth,efh->etf', x, w1)
        g = jax.nn.gelu(h, approximate=True)
        out = jnp.einsum('etf,efh->eth', g, w2)
        return out

    def _L0_attn_ref(h_t, W_DQ, b_DQ, W_UQ, b_UQ, W_DKV, b_DKV, W_UK, b_UK, W_UV, b_UV, W_QR, b_QR, W_KR, b_KR, W_O, b_O):
        import jax, jax.numpy as jnp
        import numpy as np
        import math
        D_MODEL, N_HEADS, D_K, D_C, D_HR = (256, 8, 128, 32, 32)
        B, S = (4, 512)
        b, s, _ = h_t.shape
        c_q = h_t @ W_DQ + b_DQ
        c_kv = h_t @ W_DKV + b_DKV
        q_c = (c_q @ W_UQ + b_UQ).reshape(b, s, N_HEADS, D_K).transpose(0, 2, 1, 3)
        k_c = (c_kv @ W_UK + b_UK).reshape(b, s, N_HEADS, D_K).transpose(0, 2, 1, 3)
        v_c = (c_kv @ W_UV + b_UV).reshape(b, s, N_HEADS, D_K).transpose(0, 2, 1, 3)
        q_r = (c_q @ W_QR + b_QR).reshape(b, s, N_HEADS, D_HR).transpose(0, 2, 1, 3)
        k_r = (h_t @ W_KR + b_KR)[:, None, :, :]
        k_r = jnp.broadcast_to(k_r, (b, N_HEADS, s, D_HR))
        q = jnp.concatenate([q_c, q_r], axis=-1)
        k = jnp.concatenate([k_c, k_r], axis=-1)
        scale = 1.0 / math.sqrt(D_K + D_HR)
        scores = jnp.einsum('bhsd,bhtd->bhst', q, k) * scale
        attn = jax.nn.softmax(scores, axis=-1)
        o = jnp.einsum('bhst,bhtd->bhsd', attn, v_c)
        o = o.transpose(0, 2, 1, 3).reshape(b, s, N_HEADS * D_K)
        return o @ W_O + b_O

    def _L0_ffn_ref(x, gate_w, we_gate, we_up, we_down, sw_gate, sw_up, sw_down):
        import jax, jax.numpy as jnp
        import numpy as np
        H = 256
        D = 688
        E = 8
        TOP_K = 2

        def _moe_ffn(x, gate_w, we_gate, we_up, we_down, sw_gate, sw_up, sw_down):
            B, S, h = x.shape
            xt = x.reshape(-1, h)
            T = xt.shape[0]
            logits = xt @ gate_w.T
            probs = jax.nn.softmax(logits, axis=-1)
            topk_w, topk_idx = jax.lax.top_k(probs, TOP_K)
            topk_w = topk_w / (jnp.sum(topk_w, axis=-1, keepdims=True) + 1e-20)
            cw = jnp.zeros((T, E), dtype=xt.dtype).at[jnp.arange(T)[:, None], topk_idx].add(topk_w)
            g = jnp.einsum('th,ehd->etd', xt, we_gate)
            u = jnp.einsum('th,ehd->etd', xt, we_up)
            hidden = jax.nn.silu(g) * u
            eo = jnp.einsum('etd,edh->eth', hidden, we_down)
            y = jnp.einsum('te,eth->th', cw, eo)
            y = y + jax.nn.silu(xt @ sw_gate) * (xt @ sw_up) @ sw_down
            return y.reshape(B, S, h)
        return _moe_ffn(x, gate_w, we_gate, we_up, we_down, sw_gate, sw_up, sw_down)

    def _L1_xattn_ref(values, keys, queries, mask, w_out, b_out):
        import jax, jax.numpy as jnp
        import numpy as np
        import math
        EMBED = 256
        HEADS = 16
        HEAD_DIM = EMBED // HEADS
        WINDOW = 128
        B, S = (2, 512)
        N, q_len = (queries.shape[0], queries.shape[1])
        v = values.reshape(N, -1, HEADS, HEAD_DIM)
        k = keys.reshape(N, -1, HEADS, HEAD_DIM)
        q = queries.reshape(N, -1, HEADS, HEAD_DIM)
        energy = jnp.einsum('nqhd,nkhd->nhqk', q, k)
        energy = jnp.where(mask == 0, jnp.float32(-1e+20), energy)
        attn = jax.nn.softmax(energy / math.sqrt(EMBED), axis=3)
        out = jnp.einsum('nhql,nlhd->nqhd', attn, v).reshape(N, q_len, HEADS * HEAD_DIM)
        return out @ w_out.T + b_out

    def _L1_attn_ref(x, Wq, bq, Wk, bk, Wv, bv):
        import jax, jax.numpy as jnp
        import numpy as np
        EPS = 1e-08

        def unit_projection(x):
            f = jnp.fft.fft(x)
            f = f / (jnp.abs(f) + EPS)
            return jnp.fft.ifft(f).real

        def bind(a, b):
            return jnp.fft.ifft(jnp.fft.fft(a) * jnp.fft.fft(b)).real

        def unbind(s, a):
            return jnp.fft.ifft(jnp.fft.fft(s) * jnp.conj(jnp.fft.fft(a))).real
        query = unit_projection(jnp.einsum('bsd,ed->bse', x, Wq) + bq)
        keys = unit_projection(jnp.einsum('bsd,ed->bse', x, Wk) + bk)
        values = unit_projection(jnp.einsum('bsd,ed->bse', x, Wv) + bv)
        x_k = bind(keys, values)
        s = jnp.cumsum(x_k, axis=1)
        out = unbind(s, query)
        return out

    def _L1_ffn_ref(hidden_states, sim_matrix, gates, q_proj, k_proj, v_proj, o_proj):
        import jax, jax.numpy as jnp
        import numpy as np
        HIDDEN = 256
        HEAD_DIM = 64
        N_EXPERTS = 16
        MIN_EXPERTS = 2
        B, T = (4, 512)

        def _normalize(x, axis):
            n = jnp.sqrt(jnp.sum(x * x, axis=axis, keepdims=True))
            return x / jnp.maximum(n, 1e-12)

        def _ste(x):
            hard = jax.lax.stop_gradient((x > 0).astype(x.dtype))
            return hard + x - jax.lax.stop_gradient(x)

        def _gating(hidden_states, sim_matrix, gates):
            b, t, c = hidden_states.shape
            flat = hidden_states.reshape(b * t, c)
            logits = _normalize(flat, -1) @ _normalize(sim_matrix, 0) - jax.nn.sigmoid(gates)
            gated = jax.nn.relu(logits)
            mask = _ste(gated)
            inactive = jnp.sum(mask, axis=1) == 0
            _, fb_idx = jax.lax.top_k(logits, MIN_EXPERTS)
            fb = jnp.zeros_like(mask).at[jnp.arange(b * t)[:, None], fb_idx].set(1.0)
            fb_applied = inactive[:, None] & (fb > 0)
            mask = jnp.where(fb_applied, 1.0, mask)
            masked_logits = jnp.where(mask > 0, gated, -jnp.inf)
            return jax.nn.softmax(masked_logits, axis=-1).reshape(b, t, -1)
        b, t, c = hidden_states.shape
        rw = _gating(hidden_states, sim_matrix, gates)
        q = jnp.einsum('bte,bted->btd', rw, jnp.einsum('btc,ecd->bted', hidden_states, q_proj))
        k = jnp.einsum('bte,bted->btd', rw, jnp.einsum('btc,ecd->bted', hidden_states, k_proj))
        v = jnp.einsum('bte,bted->btd', rw, jnp.einsum('btc,ecd->bted', hidden_states, v_proj))
        scale = 1.0 / jnp.sqrt(jnp.asarray(HEAD_DIM, dtype=q.dtype))
        scores = jnp.einsum('bqd,bkd->bqk', q, k) * scale
        causal = jnp.tril(jnp.ones((t, t), dtype=bool))
        scores = jnp.where(causal, scores, -jnp.inf)
        attn = jnp.einsum('bqk,bkd->bqd', jax.nn.softmax(scores, axis=-1), v)
        mixed = attn[:, :, None, :] * rw[..., None]
        return jnp.einsum('bted,edc->btc', mixed, o_proj)
    x = x + _L0_xattn_ref(_layernorm(x, axis=-1), ctx_1024, ctx_1024)
    x = x + _L0_attn_ref(_layernorm(x, axis=-1), L0_attn_W_DQ, L0_attn_b_DQ, L0_attn_W_UQ, L0_attn_b_UQ, L0_attn_W_DKV, L0_attn_b_DKV, L0_attn_W_UK, L0_attn_b_UK, L0_attn_W_UV, L0_attn_b_UV, L0_attn_W_QR, L0_attn_b_QR, L0_attn_W_KR, L0_attn_b_KR, L0_attn_W_O, L0_attn_b_O)
    x = x + _L0_ffn_ref(_layernorm(x, axis=-1), L0_ffn_gate_w, L0_ffn_we_gate, L0_ffn_we_up, L0_ffn_we_down, L0_ffn_sw_gate, L0_ffn_sw_up, L0_ffn_sw_down)
    x = x + _L1_xattn_ref(ctx_1024, ctx_1024, _layernorm(x, axis=-1), mask_1x1xSxS2_ik0, L1_xattn_w_out, L1_xattn_b_out)
    x = x + _L1_attn_ref(_layernorm(x, axis=-1), L1_attn_Wq, L1_attn_bq, L1_attn_Wk, L1_attn_bk, L1_attn_Wv, L1_attn_bv)
    x = x + _L1_ffn_ref(_layernorm(x, axis=-1), L1_ffn_sim_matrix, L1_ffn_gates, L1_ffn_q_proj, L1_ffn_k_proj, L1_ffn_v_proj, L1_ffn_o_proj)
    return x

_drawn_inputs = setup_inputs


def setup_inputs(seed=0):
    import zlib

    import numpy as np

    out = dict(_drawn_inputs(seed))
    spreads = {'L1_xattn_b_out': (0.0, 1.471), 'L1_ffn_gates': (0.0, 0.8)}
    factors = {'L0_attn_W_DQ': 8.0,
     'L0_attn_b_DQ': 8.0,
     'L0_attn_W_UQ': 8.0,
     'L0_attn_b_UQ': 8.0,
     'L0_attn_W_DKV': 5.3,
     'L0_attn_b_DKV': 8.0,
     'L0_attn_W_UK': 8.0,
     'L0_attn_b_UK': 200.0,
     'L0_attn_W_UV': 5.785,
     'L0_attn_b_UV': 7.333,
     'L0_attn_W_QR': 8.0,
     'L0_attn_b_QR': 8.0,
     'L0_attn_W_KR': 8.0,
     'L0_attn_b_KR': 200.0,
     'L0_attn_W_O': 4.408,
     'L0_attn_b_O': 8.0,
     'L0_ffn_gate_w': 8.0,
     'L0_ffn_we_gate': 8.0,
     'L0_ffn_we_up': 8.0,
     'L0_ffn_we_down': 8.0,
     'L0_ffn_sw_gate': 8.0,
     'L0_ffn_sw_up': 8.0,
     'L0_ffn_sw_down': 8.0,
     'L1_xattn_w_out': 64.0,
     'L1_attn_bk': 3.856,
     'L1_attn_bv': 3.592,
     'L1_ffn_sim_matrix': 4.655,
     'L1_ffn_q_proj': 8.0,
     'L1_ffn_k_proj': 8.0,
     'L1_ffn_v_proj': 4.459,
     'L1_ffn_o_proj': 4.435,
     'L1_attn_bq': 3.951}
    for name, (base, spread) in spreads.items():
        noise = np.random.default_rng([zlib.crc32(name.encode()), seed]).standard_normal(out[name].shape)
        drawn = base * np.exp(spread * noise) if base else spread * noise
        out[name] = jnp.asarray(drawn.astype(out[name].dtype))
    for name, factor in factors.items():
        out[name] = (out[name] * factor).astype(out[name].dtype)
    return out
```

```python
from contextlib import ExitStack

import numpy as np

import concourse.bass as bass
from concourse import mybir

ALU = mybir.AluOpType
ACT = mybir.ActivationFunctionType
AX = mybir.AxisListType
F32 = mybir.dt.float32
BF16 = mybir.dt.bfloat16
I32 = mybir.dt.int32

P = 128
B, S, D = 2, 256, 256
T = B * S
TT = T // P
DC = D // P
CTX = 4096
QT = S // P

CH = 512
NCH = B * CTX // CH
TURNS1 = NCH // 2
TPB = TURNS1 // B

H2, DK, DCQ, DR = 8, 128, 32, 32
UNITS2 = H2 * B

E3, F3, TOP = 8, 688, 2
FT = (F3 + P - 1) // P
FLAST = F3 - (FT - 1) * P

H4, DH4 = 16, 16
U4 = B * H4
TERMS = 6
KROWS = TERMS * DH4
KALL = KROWS + 3
GROUPS = 8
KT4 = CTX // P
RING = 4
MAXES = 2 * GROUPS
MAX_PLAN = (3, 3, 3, 3, 2, 2, 0, 0)
MASKED = -float((np.float32(1e20).view(np.uint32) & np.uint32(0xFFFF0000)).view(np.float32))
K_PARTS = (0, 0, 0, 1, 1, 2)
Q_PARTS = (0, 1, 2, 0, 1, 0)

NF = D // 2 + 1

E6, HD6 = 16, 64
QKV = 3 * HD6

N_CONST = 6
N_W2 = 15
N_W5 = 9
N_W6 = 9
EPS = 1e-5
SCALE2 = float((DK + DR) ** -0.5)
SCALE4 = float(D) ** -0.5
SCALE6 = float(HD6) ** -0.5


class Arena:

    def __init__(self, tensor):
        self.t, self.at = tensor, 0

    def take(self, shape, dt=F32, parts=(0, P), at=None):
        if at is not None:
            self.at = at
        size = 2 if dt == BF16 else 4
        n = int(np.prod(shape)) * size
        n = (n + 3) // 4 * 4
        v = self.t[parts[0]:parts[1], self.at // 4:(self.at + n) // 4]
        self.at += n
        assert self.at <= self.t.shape[1] * 4, (self.at, self.t.shape)
        if dt != F32:
            v = v.bitcast(dt)
        if len(shape) == 1:
            return v
        names = "abcd"[:len(shape)]
        return v.rearrange(f"p ({' '.join(names)}) -> p {' '.join(names)}",
                           **dict(zip(names[1:], shape[1:])))


class Link:

    def __init__(self, eng, sem):
        self.eng, self.sem, self.base, self.k = eng, sem, 0, 0

    def __call__(self, ins):
        self.k += 1
        ins.then_inc(self.sem, 1)
        self.eng.wait_ge(self.sem, self.base + self.k)

    def loop(self, i, per):
        self.start, self.per = self.base + self.k, per
        self.base, self.k = self.start + i * per, 0

    def end(self, turns):
        assert self.k == self.per, (self.k, self.per)
        self.base, self.k = self.start + turns * self.per, 0


def build(nc, a, out):
    ctx = ExitStack()
    with ctx:
        def sb(name, shape, dt=F32):
            return ctx.enter_context(nc.sbuf_tensor(name, shape, dt))

        def sem(name):
            return ctx.enter_context(nc.semaphore(name))

        keys_dram = nc.dram_tensor("keys_split", (3, B * D, CTX), BF16, kind="Internal").ap()

        bank = ctx.enter_context(nc.psum_tensor("bank", [P, 8, 512], F32))

        x = sb("x", [P, TT, D])
        xn = sb("xn", [P, TT, D])
        xnT = sb("xnT", [P, DC, T])
        ident = sb("ident", [P, P])
        identb = sb("identb", [P, P], BF16)
        ones = sb("ones", [P, P])
        tri = sb("tri", [P, P])
        causal = sb("causal", [P, P])
        rev = sb("rev", [P, 16])
        stats = sb("stats", [P, TT, 6])
        moments = sb("moments", [P, TT, 2])
        var_eps = sb("var_eps", [P, TT])
        rstd = sb("rstd", [P, TT])
        minus_half = sb("minus_half", [P, TT])
        gate3 = sb("gate3", [P, DC, E3])
        bdown = sb("bdown", [96, 1])
        bq2 = sb("bq2", [P, H2])
        bk2 = sb("bk2", [P, H2])
        bqr2 = sb("bqr2", [96, H2])
        prob = sb("prob", [P, TT, 16])
        pick = sb("pick", [P, 6, TT, 16])
        red = sb("red", [P, 6, TT])
        weight = sb("weight", [P, TT, 16])
        small = sb("small", [P, 8])
        square6 = sb("square6", [P, TT + E6])
        root6 = sb("root6", [P, TT + E6])
        half = sb("half", [P, TT + E6])
        woutT = sb("woutT", [P, DC, D])

        A1 = Arena(sb("region1", [P, 16384]))
        A2 = Arena(sb("region2", [P, 12288]))
        A3 = Arena(sb("region3", [P, 16384]))

        ctx_in = [A2.take([4, D], at=0 if s == 0 else None) for s in range(2)]
        ctxT = [A2.take([DC, CH]) for s in range(2)]
        geluT = [A2.take([2, S]) for s in range(2)]
        split = [A2.take([3, DC, CH], BF16) for s in range(2)]
        rest = [A2.take([DC, CH]) for s in range(2)]
        maskN = A3.take([QT, CTX], BF16, at=0)
        maskT = A3.take([KT4, S], BF16)
        mask_raw = A3.take([QT, CTX], I32)
        v2 = A1.take([TT, H2 * DK], at=0)
        oT2 = A1.take([H2, T])
        up = A1.take([2, H2 * DK])
        bv2 = A1.take([H2 * DK])
        bo2 = A1.take([D])
        wdown = A1.take([DC, 96])
        downT = A1.take([T])
        qT2 = [A1.take([T]) for s in range(2)]
        kT2 = [A1.take([T]) for s in range(2)]
        wo2 = A3.take([H2, D], at=32768)
        qrT2 = [A3.take([T]) for s in range(2)]
        p2 = [A3.take([QT, S]) for s in range(2)]
        pT2 = [A3.take([2, S]) for s in range(2)]
        sm2 = [A3.take([5, QT]) for s in range(2)]
        w3 = []
        A2.at = 0
        for s in range(2):
            w3.append((A2.take([DC, F3]), A2.take([DC, F3]), A2.take([FT, D])))
        silu = [A2.take([T]) for s in range(2)]
        hid = [A2.take([T]) for s in range(2)]
        ctx_nat = A1.take([KT4, B * D], at=0)
        qT4 = A3.take([U4, S], BF16, at=32768)
        slab = [A3.take([CTX], BF16), A3.take([CTX], BF16), A2.take([CTX], BF16, at=0), A2.take([CTX], BF16)]
        vaug = [A2.take([KT4, 32]) for s in range(2)]
        at = A2.at
        q_rows = A2.take([TT, H4, KROWS], BF16)
        q_rest = A2.take([TT, D])
        prob4 = [A2.take([4, S], at=at if s == 0 else None) for s in range(2)]
        junk = [A2.take([CH], BF16) for q in range(QT)]
        pv_sb = A2.take([S])
        o4 = A2.take([QT, B * D])
        o4T = A2.take([DC, T])
        bo4 = A2.take([D])
        cmax = A2.take([QT, GROUPS])
        negmax = A2.take([2, QT])
        negparts = A2.take([QT, 4], BF16)
        osum = A2.take([QT, 17])
        orec = A2.take([QT])
        wout = sb("wout", [P, DC, D])
        w5 = A3.take([3, DC, D], at=0)
        b5 = A3.take([3, DC])
        dft = A3.take([DC, 2 * NF])
        idft = A3.take([DC, D])
        idft_ny = A3.take([D])
        fold = A3.take([3, DC, 2 * NF])
        brow = A3.take([3, 2 * NF])
        spec = A3.take([3, TT, 2 * NF])
        mag = A3.take([TT, 2 * NF])
        magr = A3.take([3, TT, NF])
        z5 = A3.take([TT, 2 * NF])
        t5 = A3.take([TT, 2 * NF])
        o5T = A3.take([DC, T])
        o5n = A3.take([T])
        w6 = A1.take([DC, E6, QKV], at=0)
        wo6 = A1.take([E6 * HD6 // P, D])
        sim6 = A1.take([DC, E6])
        sim2 = A1.take([DC, E6])
        gates6 = A1.take([E6])
        col6 = A1.take([4, E6])
        row6 = A1.take([4, TT])
        sq6 = A1.take([TT, D])
        logit6 = A1.take([TT, E6])
        qkv = A1.take([TT, QKV])
        qT6 = A1.take([T])
        kT6 = A1.take([T])
        p6 = A1.take([TT, S])
        pT6 = A1.take([TT, 2, P])
        mixed = [A1.take([E6 * HD6]) for s in range(2)]
        mixT = [A2.take([E6 * HD6 // P, P], at=0 if s == 0 else None) for s in range(2)]

        in_x, in_const, in_mask = sem("in_x"), sem("in_const"), sem("in_mask")
        dve_link, pool_link, act_link = sem("dve_link"), sem("pool_link"), sem("act_link")
        setup, identb_ready = sem("setup"), sem("identb_ready")
        ln_var, ln_rstd, xn_ready, xnT_psum, xnT_ready = (
            sem("ln_var"), sem("ln_rstd"), sem("xn_ready"), sem("xnT_psum"), sem("xnT_ready"))
        mask_ready, maskT_psum, maskT_ready = sem("mask_ready"), sem("maskT_psum"), sem("maskT_ready")
        ctx_loaded = [sem(f"ctx_loaded{s}") for s in range(2)]
        ctxT_psum, ctxT_ready = sem("ctxT_psum"), sem("ctxT_ready")
        h1_ready, gelu_ready, out1_pair, x_added1 = (
            sem("h1_ready"), sem("gelu_ready"), sem("out1_pair"), sem("x_added1"))
        rest_ready, stored = sem("rest_ready"), [sem(f"stored{s}") for s in range(2)]
        in_w2, in_wo2 = sem("in_w2"), sem("in_wo2")
        down_psum, down_ready = sem("down_psum"), sem("down_ready")
        v2_psum, v2_ready = sem("v2_psum"), sem("v2_ready")
        proj2_psum, proj2_ready = sem("proj2_psum"), sem("proj2_ready")
        score2, nmax2, exp2, norm2 = sem("score2"), sem("nmax2"), sem("exp2"), sem("norm2")
        pT2_psum, pT2_ready = sem("pT2_psum"), sem("pT2_ready")
        o2_psum, o2_ready, y2_psum = sem("o2_psum"), sem("o2_ready"), sem("y2_psum")
        high_ready, mid_ready, low_ready = sem("high_ready"), sem("mid_ready"), sem("low_ready")
        logit3_psum, slab_ones, o4_unit = sem("logit3_psum"), sem("slab_ones"), sem("o4_unit")
        in_w3 = [sem(f"in_w3_{s}") for s in range(2)]
        logit3, exp3 = sem("logit3"), sem("exp3")
        gate_psum, up_psum, silu_ready, hid_ready, hid_used = (
            sem("gate_psum"), sem("up_psum"), sem("silu_ready"), sem("hid_ready"), sem("hid_used"))
        y3_psum, y3_added = sem("y3_psum"), sem("y3_added")
        in_ctx, in_wout = sem("in_ctx"), sem("in_wout")
        q_rows_ready, qT_psum, qT_ready = sem("q_rows_ready"), sem("qT_psum"), sem("qT_ready")
        slab_loaded = [sem(f"slab_loaded{s}") for s in range(RING)]
        v_ready = sem("v_ready")
        score4, exp4_ready = sem("score4"), sem("exp4_ready")
        max_psum, max_taken, negmax_ready, negT_psum, negT_ready = (
            sem("max_psum"), sem("max_taken"), sem("negmax_ready"), sem("negT_psum"), sem("negT_ready"))
        pv_psum, pv_copied, oT_psum, oT_used = (
            sem("pv_psum"), sem("pv_copied"), sem("oT_psum"), sem("oT_used"))
        o4_ready, o4T_psum, o4T_ready, y4_psum = (
            sem("o4_ready"), sem("o4T_psum"), sem("o4T_ready"), sem("y4_psum"))
        wout_psum, wout_ready = sem("wout_psum"), sem("wout_ready")
        in_w5, fold_psum, fold_ready = sem("in_w5"), sem("fold_psum"), sem("fold_ready")
        spec_psum, spec_ready, mag_ready, root_ready = (
            sem("spec_psum"), sem("spec_ready"), sem("mag_ready"), sem("root_ready"))
        z_ready, sum_psum, o5_ready, o5T_psum, o5T_ready, y5_psum = (
            sem("z_ready"), sem("sum_psum"), sem("o5_ready"), sem("o5T_psum"), sem("o5T_ready"), sem("y5_psum"))
        in_w6, sim_sq, logit6_psum, gate_arg, gate_exp = (
            sem("in_w6"), sem("sim_sq"), sem("logit6_psum"), sem("gate_arg"), sem("gate_exp"))
        pow_arg, pow_ready, exp6w_arg, exp6w = sem("pow_arg"), sem("pow_ready"), sem("exp6w_arg"), sem("exp6w")
        proj6, proj6_used, qk6_psum, qk6_ready = sem("proj6"), sem("proj6_used"), sem("qk6_psum"), sem("qk6_ready")
        qkv_ready, score6, nmax6, exp6, norm6 = (
            sem("qkv_ready"), sem("score6"), sem("nmax6"), sem("exp6"), sem("norm6"))
        pT6_psum, pT6_ready, att6 = sem("pT6_psum"), sem("pT6_ready"), sem("att6")
        mix_ready, mixT_psum, mixT_ready, y6_psum = (
            sem("mix_ready"), sem("mixT_psum"), sem("mixT_ready"), sem("y6_psum"))
        x_final, out_stored = sem("x_final"), sem("out_stored")

        block = ctx.enter_context(nc.Block())

        def bf16_bank(n):
            return bank[:, n, :].bitcast(BF16)

        def cols(t, start, n=P):
            return slice(start, start + n)

        @block.sync
        def _(sp):
            sp.dma_start(x[:, :, :], a["x"].rearrange("b (t p) d -> p (b t) d", p=P)).then_inc(in_x, 16)
            for dst, name in ((ident, "c_ident"), (tri, "c_tri"), (causal, "c_causal")):
                sp.dma_start(dst[:, :], a[name]).then_inc(in_const, 16)
            sp.dma_start(rev[:, :], a["c_rev"].partition_broadcast(P)).then_inc(in_const, 16)

            chunks = a["ctx_1024"].rearrange("b (c t p) d -> (b c) p t d", t=4, p=P)

            def load_chunk(s, c):
                sp.dma_start(ctx_in[s], chunks[bass.ds(c, 1)].rearrange("o p t d -> p (o t) d"))\
                  .then_inc(ctx_loaded[s], 16)
            for s in range(2):
                load_chunk(s, s)
            sp.dma_start(mask_raw, a["mask_1x1xSxS2_ik0"].rearrange("a b (t p) k -> p (a b t) k", p=P))\
              .then_inc(in_mask, 16)
            for c in range(DC):
                sp.dma_start(gate3[:, c, :], a["L0_ffn_gate_w"][:, c * P:(c + 1) * P].rearrange("e p -> p e"),
                             allow_slow_non_contiguous=True)\
                  .then_inc(in_const, 16)
            for n, name in enumerate(("DQ", "DKV", "KR")):
                sp.dma_start(bdown[32 * n:32 * n + 32, :], a["L0_attn_b_" + name].rearrange("(p o) -> p o", o=1),
                             allow_slow_non_contiguous=True)\
                  .then_inc(in_w2, 16)
                sp.dma_start(wdown[:, :, 32 * n:32 * n + 32],
                             a["L0_attn_W_" + name].rearrange("(c p) n -> p c n", p=P)).then_inc(in_w2, 16)
            sp.dma_start(bq2[:, :], a["L0_attn_b_UQ"].rearrange("(h p) -> p h", p=P), allow_slow_non_contiguous=True).then_inc(in_w2, 16)
            sp.dma_start(bk2[:, :], a["L0_attn_b_UK"].rearrange("(h p) -> p h", p=P), allow_slow_non_contiguous=True).then_inc(in_w2, 16)
            sp.dma_start(bqr2[64:96, :], a["L0_attn_b_QR"].rearrange("(h p) -> p h", p=DR), allow_slow_non_contiguous=True).then_inc(in_w2, 16)
            sp.dma_start(up[0:32, 0, :], a["L0_attn_W_UQ"]).then_inc(in_w2, 16)
            sp.dma_start(up[0:32, 1, 0:H2 * DR], a["L0_attn_W_QR"]).then_inc(in_w2, 16)
            sp.dma_start(up[32:64, 0, :], a["L0_attn_W_UK"]).then_inc(in_w2, 16)
            sp.dma_start(up[32:64, 1, :], a["L0_attn_W_UV"]).then_inc(in_w2, 16)
            sp.dma_start(bv2, a["L0_attn_b_UV"].partition_broadcast(P)).then_inc(in_w2, 16)
            sp.dma_start(bo2, a["L0_attn_b_O"].partition_broadcast(P)).then_inc(in_w2, 16)
            sp.dma_start(wout[:, :, :], a["L1_xattn_w_out"].rearrange("(c p) n -> p c n", p=P)).then_inc(in_wout, 16)
            with sp.Fori(0, TURNS1 - 1) as i:
                for s in range(2):
                    sp.wait_ge(out1_pair, 4 * i + 2 * s + 2)
                    load_chunk(s, 2 * i + s + 2)

            sp.wait_ge(mask_ready, QT)
            sp.dma_start(wo2, a["L0_attn_W_O"].rearrange("(h p) n -> p h n", p=P)).then_inc(in_wo2, 16)

            def load_expert(s, gate, upw, down):
                g, u, d = w3[s]
                sp.dma_start(g, gate.rearrange("(c p) n -> p c n", p=P)).then_inc(in_w3[s], 16)
                sp.dma_start(u, upw.rearrange("(c p) n -> p c n", p=P)).then_inc(in_w3[s], 16)
                sp.dma_start(d[:, 0:FT - 1, :], down[0:(FT - 1) * P, :].rearrange("(c p) n -> p c n", p=P))\
                  .then_inc(in_w3[s], 16)
                sp.dma_start(d[0:FLAST, FT - 1, :], down[(FT - 1) * P:F3, :]).then_inc(in_w3[s], 16)

            def routed(e):
                return [a[n][bass.ds(e, 1)].rearrange("o a b -> (o a) b")
                        for n in ("L0_ffn_we_gate", "L0_ffn_we_up", "L0_ffn_we_down")]
            for s in range(2):
                sp.wait_ge(stored[s], 48 * TURNS1)
            sp.wait_ge(x_added1, TURNS1 + 1)
            load_expert(0, a["L0_ffn_sw_gate"], a["L0_ffn_sw_up"], a["L0_ffn_sw_down"])
            load_expert(1, *routed(0))
            sp.wait_ge(xn_ready, 3)
            for b in range(B):
                sp.dma_start(ctx_nat[:, :, b * D:(b + 1) * D],
                             a["ctx_1024"][b].rearrange("(t p) d -> p t d", p=P)).then_inc(in_ctx, 16)

            def load_slab(s, u):
                for n, part in enumerate(K_PARTS):
                    sp.dma_start(slab[s][n * DH4:(n + 1) * DH4, :],
                                 keys_dram[part, bass.ds(u * DH4, DH4), :]).then_inc(slab_loaded[s], 16)
            for s in range(2):
                load_slab(s, s)
            with sp.Fori(0, E3 // 2 - 1) as i:
                sp.wait_ge(y3_psum, 2 * i + 1)
                load_expert(0, *routed(2 * i + 1))
                sp.wait_ge(y3_psum, 2 * i + 2)
                load_expert(1, *routed(2 * i + 2))
            sp.wait_ge(y3_psum, E3 - 1)
            load_expert(0, *routed(E3 - 1))

            sp.wait_ge(xn_ready, 4)
            sp.dma_start(bo4, a["L1_xattn_b_out"].partition_broadcast(P)).then_inc(in_wout, 16)
            for s in range(2, RING):
                load_slab(s, s)
            with sp.Fori(0, U4 // RING - 1) as i:
                for s in range(RING):
                    sp.wait_ge(score4, GROUPS * RING * i + GROUPS * (s + 1))
                    load_slab(s, RING * i + s + RING)
            sp.wait_ge(score4, GROUPS * U4)
            sp.wait_ge(max_taken, MAXES * U4)
            for n, name in enumerate("kvq"):
                sp.dma_start(w5[:, n, :, :], a["L1_attn_W" + name].rearrange("(c p) n -> p c n", p=P)).then_inc(in_w5, 16)
                sp.dma_start(b5[:, n, :], a["L1_attn_b" + name].rearrange("(c p) -> p c", p=P), allow_slow_non_contiguous=True).then_inc(in_w5, 16)
            sp.dma_start(dft, a["c_dft"].rearrange("(c p) n -> p c n", p=P)).then_inc(in_w5, 16)
            sp.dma_start(idft, a["c_idft"][0:D, :].rearrange("(c p) n -> p c n", p=P)).then_inc(in_w5, 16)
            sp.dma_start(idft_ny[0:1, :], a["c_idft"][D:D + 1, :]).then_inc(in_w5, 16)
            sp.wait_ge(v_ready, U4)
            for n, name in enumerate("qkv"):
                for c in range(DC):
                    sp.dma_start(w6[:, c, :, n * HD6:(n + 1) * HD6],
                                 a[f"L1_ffn_{name}_proj"][:, c * P:(c + 1) * P, :].rearrange("e p d -> p e d"))\
                      .then_inc(in_w6, 16)
            sp.dma_start(wo6, a["L1_ffn_o_proj"].rearrange("e d n -> (e d) n").rearrange("(j p) n -> p j n", p=P))\
              .then_inc(in_w6, 16)
            sp.dma_start(sim6, a["L1_ffn_sim_matrix"].rearrange("(c p) e -> p c e", p=P)).then_inc(in_w6, 16)
            sp.dma_start(gates6, a["L1_ffn_gates"].partition_broadcast(P)).then_inc(in_w6, 16)
            sp.wait_ge(x_final, 1)
            sp.dma_start(out.rearrange("b (t p) d -> p (b t) d", p=P), x[:, :, :]).then_inc(out_stored, 16)
            sp.wait_ge(out_stored, 16)

        @block.gpsimd
        def _(pool):
            link = Link(pool, pool_link)
            nc.gpsimd.memset(minus_half[:, :], -0.5).then_inc(setup, 1)
            nc.gpsimd.memset(half[:, :], 0.5).then_inc(setup, 1)
            nc.gpsimd.memset(ones[:, :], 1.0).then_inc(setup, 1)
            pool.wait_ge(setup, 3)

            def inverse_root(n):
                pool.wait_ge(ln_var, n + 1)
                nc.gpsimd.tensor_tensor(out=rstd[:, :], in0=var_eps[:, :], in1=minus_half[:, :], op=ALU.pow)\
                  .then_inc(ln_rstd, 1)

            def carry_wait():
                nc.gpsimd.tensor_tensor(out=small[0:1, 3:4], in0=half[0:1, 0:1], in1=half[0:1, 0:1], op=ALU.add)

            inverse_root(0)
            pool.wait_ge(in_mask, 16)
            for t in range(QT):
                nc.gpsimd.tensor_scalar(maskN[:, t, :], mask_raw[:, t, :], 0.0, MASKED, ALU.is_equal, ALU.mult)\
                  .then_inc(mask_ready, 1)
            with pool.Fori(0, B) as b:
                with pool.Fori(0, TPB) as j:
                    i = b * TPB + j
                    for s in range(2):
                        pool.wait_ge(rest_ready, 2 * i + s + 1)
                        carry_wait()
                        nc.gpsimd.tensor_copy(split[s][:, 1, :, :], rest[s]).then_inc(mid_ready, 1)
                        pool.wait_ge(mid_ready, 2 * i + s + 1)
                        nc.gpsimd.tensor_tensor(out=split[s][:, 2, :, :], in0=rest[s], in1=split[s][:, 1, :, :],
                                                op=ALU.subtract).then_inc(low_ready, 1)
                        pool.wait_ge(low_ready, 2 * i + s + 1)
                        for part in range(3):
                            pool.dma_start(
                                keys_dram[part, bass.ds(b * D, D), bass.ds((2 * j + s) * CH, CH)]
                                .rearrange("(c p) f -> p c f", p=P),
                                split[s][:, part, :, :]).then_inc(stored[s], 16)
            for n in range(1, 4):
                inverse_root(n)
            pool.wait_ge(xn_ready, 4)
            for s in range(2):
                link(nc.gpsimd.memset(vaug[s], 0.0))
                link(nc.gpsimd.memset(vaug[s][:, :, DH4:DH4 + 1], 1.0))
            for s in range(RING):
                nc.gpsimd.memset(slab[s][KROWS:KALL, :], 1.0).then_inc(slab_ones, 1)
                pool.wait_ge(slab_ones, s + 1)
            pool.wait_ge(in_ctx, 32)
            for u in range(2):
                nc.gpsimd.tensor_copy(vaug[u][:, :, 0:DH4], ctx_nat[:, :, u * DH4:(u + 1) * DH4])\
                  .then_inc(v_ready, 1)
            with pool.Fori(0, U4 // 2 - 1) as i:
                for s in range(2):
                    pool.wait_ge(v_ready, 2 * i + s + 2)
                    pool.wait_ge(pv_psum, 2 * i + s + 1)
                    carry_wait()
                    nc.gpsimd.tensor_copy(vaug[s][:, :, 0:DH4], ctx_nat[:, :, bass.ds((2 * i + s + 2) * DH4, DH4)])\
                      .then_inc(v_ready, 1)
            inverse_root(4)
            inverse_root(5)
            pool.wait_ge(pow_arg, 1)
            nc.gpsimd.tensor_tensor(out=root6[:, :], in0=square6[:, :], in1=half[:, :], op=ALU.pow)\
              .then_inc(pow_ready, 1)

        @block.scalar
        def _(act):
            def norm_out(n):
                act.wait_ge(xnT_psum, n + 1)
                nc.scalar.activation(xnT[:, :, :], bank[:, 0:2, :], ACT.Copy).then_inc(xnT_ready, 1)

            norm_out(0)
            with act.Fori(0, TURNS1) as i:
                for s in range(2):
                    act.wait_ge(ctxT_psum, 2 * i + s + 1)
                    if s == 0:
                        act.wait_ge(x_added1, i + 1)
                    nc.scalar.activation(ctxT[s], bank[:, 6 * s:6 * s + 2, :], ACT.Copy).then_inc(ctxT_ready, 1)
                for s in range(2):
                    for p in range(2):
                        act.wait_ge(h1_ready, 4 * i + 2 * s + p + 1)
                        nc.scalar.activation(geluT[p].rearrange("p a b -> p (a b)"), bank[:, 2 + p, :],
                                             ACT.Gelu_apprx_tanh).then_inc(gelu_ready, 1)
            for g in range(GROUPS * 2):
                act.wait_ge(maskT_psum, g + 1)
                nc.scalar.activation(maskT[:, 2 * g:2 * g + 2, :].rearrange("p a b -> p (a b)"),
                                     bf16_bank(2 + g % 2)[:, 0:512], ACT.Copy).then_inc(maskT_ready, 1)
            act.wait_ge(wout_psum, 1)
            nc.scalar.activation(woutT[:, :, :], bank[:, 4:6, 0:D], ACT.Copy).then_inc(wout_ready, 1)

            norm_out(1)
            act.wait_ge(in_w2, 16 * N_W2)
            act.wait_ge(down_psum, 1)
            nc.scalar.activation(downT[0:96, :], bank[0:96, 2, :], ACT.Identity, bias=bdown[:, :])\
              .then_inc(down_ready, 1)

            def heads_out(h):
                s = h % 2
                act.wait_ge(proj2_psum, h + 1)
                nc.scalar.activation(qT2[s], bank[:, 3, :], ACT.Identity, bias=bq2[:, h:h + 1])
                nc.scalar.activation(kT2[s], bank[:, 4, :], ACT.Identity, bias=bk2[:, h:h + 1])
                nc.scalar.activation(qrT2[s][64:96, :], bank[64:96, 5, :], ACT.Identity,
                                     bias=bqr2[64:96, h:h + 1]).then_inc(proj2_ready, 1)

            def exps(n):
                s = n % 2
                act.wait_ge(nmax2, n + 1)
                for t in range(QT):
                    e = nc.scalar.activation(p2[s][:, t, :], bank[:, 6 + s, t * S:(t + 1) * S], ACT.Exp,
                                             bias=sm2[s][:, 1, t:t + 1], scale=SCALE2,
                                             accum_out=sm2[s][:, 2, t:t + 1])
                e.then_inc(exp2, 1)

            heads_out(0)
            exps(0)
            for n in range(UNITS2):
                if n + 1 < UNITS2:
                    if (n + 1) % B == 0:
                        heads_out((n + 1) // B)
                    exps(n + 1)
                act.wait_ge(o2_psum, n + 1)
                nc.scalar.activation(oT2[:, n // B, (n % B) * S:(n % B + 1) * S], bank[:, 2, 0:S], ACT.Copy)\
                  .then_inc(o2_ready, 1)

            norm_out(2)
            act.wait_ge(logit3, 1)
            nc.scalar.activation(prob[:, :, 0:E3], prob[:, :, 0:E3], ACT.Exp).then_inc(exp3, 1)

            def silus(k0):
                for f in range(FT):
                    m = P if f < FT - 1 else FLAST
                    act.wait_ge(gate_psum, k0 + f + 1)
                    nc.scalar.activation(silu[f % 2][0:m, :], bank[0:m, f % 2, :], ACT.Silu).then_inc(silu_ready, 1)
            silus(0)
            with act.Fori(0, E3 // 2) as i:
                for s in range(2):
                    silus(2 * FT * i + FT * (s + 1))

            norm_out(3)
            for n in range(TT * 2):
                t, half_h = n // 2, n % 2
                act.wait_ge(qT_psum, n + 1)
                u0 = (t // QT) * H4 + half_h * 8
                nc.scalar.activation(qT4[0:KROWS, u0:u0 + 8, (t % QT) * P:(t % QT + 1) * P],
                                     bf16_bank(2 + n % 2)[0:KROWS, :].rearrange("p (h q) -> p h q", h=8),
                                     ACT.Copy).then_inc(qT_ready, 1)

            def softmax_numerators(n0):
                for g in range(GROUPS):
                    act.wait_ge(score4, n0 + g + 1)
                    nc.scalar.activation(prob4[g % 2].rearrange("p a b -> p (a b)"),
                                         bank[:, 2 * (g % 2):2 * (g % 2) + 2, :].rearrange("p a b -> p (a b)"),
                                         ACT.Exp, scale=SCALE4).then_inc(exp4_ready, 1)
            with act.Fori(0, U4) as i:
                softmax_numerators(GROUPS * i)
            act.wait_ge(o4T_psum, 1)
            nc.scalar.activation(o4T, bank[:, 4:6, :], ACT.Copy).then_inc(o4T_ready, 1)

            norm_out(4)
            act.wait_ge(fold_psum, 1)
            for n in range(3):
                nc.scalar.activation(fold[:, n, :, :], bank[:, 2 + 2 * n:4 + 2 * n, 0:2 * NF], ACT.Copy)\
                  .then_inc(fold_ready, 1)
            act.wait_ge(fold_psum, 2)
            nc.scalar.activation(brow[0:1, :, :], bank[0:1, 2:5, 0:2 * NF], ACT.Copy).then_inc(fold_ready, 1)
            for n in range(3):
                for t in range(0, TT, 2):
                    k = n * TT + t
                    act.wait_ge(spec_psum, k + 2)
                    o = 4 * ((k // 2) % 2)
                    nc.scalar.activation(spec[:, n, t:t + 2, :], bank[:, o:o + 2, 0:2 * NF], ACT.Copy)\
                      .then_inc(spec_ready, 1)
            for n in range(3):
                act.wait_ge(mag_ready, n + 1)
                nc.scalar.activation(magr[:, n, :, :], magr[:, n, :, :], ACT.Sqrt).then_inc(root_ready, 1)
            act.wait_ge(o5T_psum, 1)
            nc.scalar.activation(o5T, bank[:, 0:2, :], ACT.Copy).then_inc(o5T_ready, 1)
            nc.scalar.activation(o5n[0:1, :], bank[0:1, 2, :], ACT.Copy).then_inc(o5T_ready, 1)

            norm_out(5)
            act.wait_ge(gate_arg, 1)
            nc.scalar.activation(col6[:, 0, :], gates6, ACT.Exp, scale=-1.0).then_inc(gate_exp, 1)
            act.wait_ge(exp6w_arg, 1)
            nc.scalar.activation(prob[:, :, :], prob[:, :, :], ACT.Exp).then_inc(exp6w, 1)
            act.wait_ge(qk6_psum, 1)
            nc.scalar.activation(qT6[0:HD6, :], bank[0:HD6, 0, :], ACT.Copy)
            nc.scalar.activation(kT6[0:HD6, :], bank[0:HD6, 1, :], ACT.Copy).then_inc(qk6_ready, 1)
            for t in range(TT):
                w = S if t % QT else P
                act.wait_ge(nmax6, t + 1)
                nc.scalar.activation(p6[:, t, 0:w], p6[:, t, 0:w], ACT.Exp, bias=row6[:, 2, t:t + 1],
                                     accum_out=row6[:, 3, t:t + 1]).then_inc(exp6, 1)
            for t in range(TT):
                act.wait_ge(mixT_psum, t + 1)
                nc.scalar.activation(mixT[t % 2], bank[:, 2 * (t % 2):2 * (t % 2) + 2, :].rearrange("p a (j q) -> p (a j) q", q=P),
                                     ACT.Copy).then_inc(mixT_ready, 1)

        @block.tensor
        def _(pe):
            mm = nc.tensor.matmul

            def norm_T(n):
                pe.wait_ge(xn_ready, n + 1)
                for t in range(TT):
                    for c in range(DC):
                        last = nc.tensor.transpose(bank[:, c, t * P:(t + 1) * P], xn[:, t, c * P:(c + 1) * P], ident[:, :])
                last.then_inc(xnT_psum, 1)
                pe.wait_ge(xnT_ready, n + 1)

            pe.wait_ge(in_const, 16 * N_CONST)
            pe.wait_ge(setup, 3)
            pe.wait_ge(identb_ready, 1)
            norm_T(0)
            with pe.Fori(0, B) as b:
                with pe.Fori(0, TPB) as j:
                    i = b * TPB + j
                    for s in range(2):
                        pe.wait_ge(ctx_loaded[s], 16 * i + 16)
                        for t in range(4):
                            for c in range(DC):
                                last = nc.tensor.transpose(bank[:, 6 * s + c, t * P:(t + 1) * P],
                                                           ctx_in[s][:, t, c * P:(c + 1) * P], ident[:, :])
                        last.then_inc(ctxT_psum, 1)
                    for s in range(2):
                        pe.wait_ge(ctxT_ready, 2 * i + s + 1)
                        for p in range(2):
                            for t in range(2):
                                f = (2 * p + t) * P
                                for c in range(DC):
                                    last = mm(bank[:, 2 + p, t * S:(t + 1) * S], ctxT[s][:, c, f:f + P],
                                              xnT[:, c, bass.ds(b * S, S)], start=(c == 0), stop=(c == DC - 1))
                            last.then_inc(h1_ready, 1)
                        if s == 0:
                            pe.wait_ge(x_added1, i + 1)
                        for p in range(2):
                            pe.wait_ge(gelu_ready, 4 * i + 2 * s + p + 1)
                            for t in range(2):
                                for q in range(QT):
                                    last = mm(bank[:, 4 + q, 0:D], geluT[p][:, t, q * P:(q + 1) * P],
                                              ctx_in[s][:, 2 * p + t, :], start=(s + p + t == 0),
                                              stop=(s + p + t == 3))
                            last.then_inc(out1_pair, 1)
            pe.wait_ge(mask_ready, QT)
            pe.wait_ge(x_added1, TURNS1 + 1)
            for g in range(GROUPS * 2):
                if g >= 2:
                    pe.wait_ge(maskT_ready, g - 1)
                for k in range(2):
                    for q in range(QT):
                        f = (2 * g + k) * P
                        last = nc.tensor.transpose(bf16_bank(2 + g % 2)[:, k * S + q * P:k * S + (q + 1) * P],
                                                   maskN[:, q, f:f + P], identb[:, :])
                last.then_inc(maskT_psum, 1)
            pe.wait_ge(in_wout, 16)
            for c in range(DC):
                for o in range(DC):
                    last = nc.tensor.transpose(bank[:, 4 + c, o * P:(o + 1) * P], wout[:, o, c * P:(c + 1) * P], ident[:, :])
            last.then_inc(wout_psum, 1)

            pe.wait_ge(maskT_ready, GROUPS * 2)
            pe.wait_ge(wout_ready, 1)
            norm_T(1)
            pe.wait_ge(in_w2, 16 * N_W2)
            for c in range(DC):
                last = mm(bank[0:96, 2, :], wdown[:, c, :], xnT[:, c, :], start=(c == 0), stop=(c == DC - 1))
            last.then_inc(down_psum, 1)
            pe.wait_ge(down_ready, 1)

            def heads(h):
                if h > 0:
                    pe.wait_ge(proj2_ready, h)
                w = slice(h * DK, (h + 1) * DK)
                mm(bank[:, 3, :], up[0:32, 0, w], downT[0:32, :], start=True, stop=True)
                mm(bank[:, 4, :], up[32:64, 0, w], downT[32:64, :], start=True, stop=True)
                mm(bank[64:96, 5, :], up[0:32, 1, h * DR:(h + 1) * DR], downT[0:32, :], start=True, stop=True)\
                    .then_inc(proj2_psum, 1)

            def scores(n):
                h, b = n // B, n % B
                if b == 0:
                    pe.wait_ge(proj2_ready, h + 1)
                for q in range(QT):
                    o = bank[:, 6 + n % 2, q * S:(q + 1) * S]
                    t = b * S + q * P
                    mm(o, qT2[h % 2][:, t:t + P], kT2[h % 2][:, b * S:(b + 1) * S], start=True, stop=False)
                    last = mm(o, qrT2[h % 2][64:96, t:t + P], downT[64:96, b * S:(b + 1) * S], start=False, stop=True)
                last.then_inc(score2, 1)

            for n in range(TT * 2):
                if n >= 2:
                    pe.wait_ge(v2_ready, n - 1)
                t, c = n // 2, n % 2
                mm(bank[:, n % 2, :], downT[32:64, t * P:(t + 1) * P], up[32:64, 1, c * 512:(c + 1) * 512],
                   start=True, stop=True).then_inc(v2_psum, 1)
            heads(0)
            scores(0)
            pe.wait_ge(v2_ready, TT * 2)
            for n in range(UNITS2):
                h, b = n // B, n % B
                if n + 1 < UNITS2:
                    if (n + 1) % B == 0:
                        heads((n + 1) // B)
                    scores(n + 1)
                pe.wait_ge(norm2, n + 1)
                for k in range(2):
                    for q in range(QT):
                        last = nc.tensor.transpose(bank[:, n % 2, k * S + q * P:k * S + (q + 1) * P],
                                                   p2[n % 2][:, q, k * P:(k + 1) * P], ident[:, :])
                last.then_inc(pT2_psum, 1)
                pe.wait_ge(pT2_ready, n + 1)
                if n > 0:
                    pe.wait_ge(o2_ready, n)
                for k in range(2):
                    last = mm(bank[:, 2, 0:S], v2[:, b * QT + k, h * DK:(h + 1) * DK], pT2[n % 2][:, k, :],
                              start=(k == 0), stop=(k == 1))
                last.then_inc(o2_psum, 1)
            pe.wait_ge(o2_ready, UNITS2)
            pe.wait_ge(in_wo2, 16)
            for t in range(TT):
                for h in range(H2):
                    last = mm(bank[:, 3 + t, 0:D], oT2[:, h, t * P:(t + 1) * P], wo2[:, h, :],
                              start=(h == 0), stop=(h == H2 - 1))
                last.then_inc(y2_psum, 1)

            norm_T(2)
            for t in range(TT):
                for c in range(DC):
                    last = mm(bank[:, 7, t * 16:t * 16 + E3], xnT[:, c, t * P:(t + 1) * P], gate3[:, c, :],
                              start=(c == 0), stop=(c == DC - 1))
            last.then_inc(logit3_psum, 1)

            def down3(s, n, f, k0):
                m = P if f < FT - 1 else FLAST
                pe.wait_ge(hid_ready, k0 + f + 1)
                if f == 0:
                    pe.wait_ge(y3_added, n)
                for t in range(TT):
                    last = mm(bank[:, 4 + t, 0:D], hid[f % 2][0:m, t * P:(t + 1) * P], w3[s][2][0:m, f, :],
                              start=(f == 0), stop=(f == FT - 1))
                if f == FT - 1:
                    last.then_inc(y3_psum, 1)

            def expert(s, n, fills):
                k0 = n * FT
                pe.wait_ge(in_w3[s], fills * 64)
                for f in range(FT):
                    m = P if f < FT - 1 else FLAST
                    for w, o, done in ((0, 0, gate_psum), (1, 2, up_psum)):
                        for c in range(DC):
                            last = mm(bank[0:m, o + f % 2, :], w3[s][w][:, c, f * P:f * P + m], xnT[:, c, :],
                                      start=(c == 0), stop=(c == DC - 1))
                        last.then_inc(done, 1)
                    if f > 0:
                        down3(s, n, f - 1, k0)
                down3(s, n, FT - 1, k0)
            expert(0, 0, 1)
            with pe.Fori(0, E3 // 2) as i:
                expert(1, 2 * i + 1, i + 1)
                expert(0, 2 * i + 2, i + 2)

            norm_T(3)
            pe.wait_ge(q_rows_ready, 1)
            for n in range(TT * 2):
                if n >= 2:
                    pe.wait_ge(qT_ready, n - 1)
                t, hh = n // 2, n % 2
                for h in range(8):
                    last = nc.tensor.transpose(bf16_bank(2 + n % 2)[0:KROWS, h * P:(h + 1) * P],
                                               q_rows[:, t, hh * 8 + h, :], identb[:, :])
                last.then_inc(qT_psum, 1)
            pe.wait_ge(qT_ready, TT * 2)
            pe.wait_ge(slab_ones, RING)

            def max_piece(s, u, m):
                q, c = m % 2, m // 2
                k = u * MAXES + m
                if not isinstance(k, int) or k >= 2:
                    pe.wait_ge(max_taken, k - 1)
                mm(bank[:, 4 + q, :], qT4[0:KROWS, bass.ds(u, 1), q * P:(q + 1) * P].rearrange("p o q -> p (o q)"),
                   slab[s][0:KROWS, c * CH:(c + 1) * CH], start=True, stop=True).then_inc(max_psum, 1)

            def negmax_T(u):
                pe.wait_ge(negmax_ready, u + 1)
                for q in range(QT):
                    last = nc.tensor.transpose(bf16_bank(7)[KROWS:KALL, q * P:(q + 1) * P], negparts[:, q, 0:3],
                                               identb[:, :])
                last.then_inc(negT_psum, 1)

            def score_group(s, u, g):
                for k in range(4):
                    mm(bank[:, 2 * (g % 2) + k // 2, (k % 2) * S:(k % 2 + 1) * S],
                       slab[s][0:KALL, (4 * g + k) * P:(4 * g + k + 1) * P],
                       qT4[0:KALL, bass.ds(u, 1), :].rearrange("p o q -> p (o q)"),
                       start=(k % 2 == 0), stop=False, skip_group_check=True)
                for k in range(2):
                    last = mm(bank[:, 2 * (g % 2) + k, :], identb[:, :],
                              maskT[:, 4 * g + 2 * k:4 * g + 2 * k + 2, :].rearrange("p a b -> p (a b)"),
                              start=False, stop=True, skip_group_check=True)
                last.then_inc(score4, 1)

            def values_group(s, n0, g):
                pe.wait_ge(exp4_ready, n0 + g + 1)
                for k in range(4):
                    last = mm(bank[32 * k:32 * k + 32, 6, 0:S], vaug[s][:, 4 * g + k, :], prob4[g % 2][:, k, :],
                              start=(g == 0), stop=(g == GROUPS - 1), skip_group_check=True)
                if g == GROUPS - 1:
                    last.then_inc(pv_psum, 1)

            def unit(s, u, fills, more):
                m = 0
                s1 = (s + 1) % RING
                if more:
                    pe.wait_ge(slab_loaded[s1], (fills + (1 if s1 == 0 else 0)) * 16 * TERMS)
                for g in range(GROUPS):
                    if g < GROUPS - 1:
                        score_group(s, u, g + 1)
                    if more:
                        for _ in range(MAX_PLAN[g]):
                            max_piece(s1, u + 1, m)
                            m += 1
                        if g == GROUPS - 1:
                            pe.wait_ge(negT_ready, u + 2)
                            score_group(s1, u + 1, 0)
                    if g == 0:
                        pe.wait_ge(v_ready, u + 1)
                        pe.wait_ge(pv_copied, u + 1)
                    values_group(s % 2, GROUPS * u, g)
                    if more and g == GROUPS - 2:
                        negmax_T(u + 1)
                pe.wait_ge(pv_copied, u + 2)
                for q in range(QT):
                    last = nc.tensor.transpose(bank[:, 7, 256 + q * P:256 + (q + 1) * P], pv_sb[:, q * P:(q + 1) * P],
                                               ident[:, :])
                last.then_inc(oT_psum, 1)

            pe.wait_ge(slab_loaded[0], 16 * TERMS)
            for m in range(MAXES):
                max_piece(0, 0, m)
            negmax_T(0)
            pe.wait_ge(negT_ready, 1)
            score_group(0, 0, 0)
            with pe.Fori(0, U4 // RING - 1) as i:
                for s in range(RING):
                    unit(s, RING * i + s, i + 1, True)
            for s in range(RING):
                unit(s, U4 - RING + s, U4 // RING, s < RING - 1)
            pe.wait_ge(o4_ready, 1)
            for t in range(TT):
                for c in range(DC):
                    o = (t // QT) * D + c * P
                    last = nc.tensor.transpose(bank[:, 4 + c, t * P:(t + 1) * P], o4[:, t % QT, o:o + P], ident[:, :])
            last.then_inc(o4T_psum, 1)
            pe.wait_ge(o4T_ready, 1)
            for t in range(TT):
                for c in range(DC):
                    last = mm(bank[:, t, 0:D], o4T[:, c, t * P:(t + 1) * P], woutT[:, c, :],
                              start=(c == 0), stop=(c == DC - 1))
                last.then_inc(y4_psum, 1)

            pe.wait_ge(in_w5, 16 * N_W5)
            norm_T(4)
            for n in range(3):
                for o in range(DC):
                    for c in range(DC):
                        last = mm(bank[:, 2 + 2 * n + o, 0:2 * NF], w5[:, n, c, o * P:(o + 1) * P], dft[:, c, :],
                                  start=(c == 0), stop=(c == DC - 1))
            last.then_inc(fold_psum, 1)
            pe.wait_ge(fold_ready, 3)
            for n in range(3):
                for c in range(DC):
                    last = mm(bank[0:1, 2 + n, 0:2 * NF], b5[:, n, c:c + 1], dft[:, c, :],
                              start=(c == 0), stop=(c == DC - 1))
            last.then_inc(fold_psum, 1)
            pe.wait_ge(fold_ready, 4)
            for n in range(3):
                for t in range(TT):
                    k = n * TT + t
                    o = bank[:, 4 * ((k // 2) % 2) + k % 2, 0:2 * NF]
                    if k >= 4 and k % 2 == 0:
                        pe.wait_ge(spec_ready, k // 2 - 1)
                    for c in range(DC):
                        mm(o, xnT[:, c, t * P:(t + 1) * P], fold[:, n, c, :], start=(c == 0), stop=False)
                    mm(o, ones[0:1, :], brow[0:1, n, :], start=False, stop=True).then_inc(spec_psum, 1)
            pe.wait_ge(spec_ready, 6)
            pe.wait_ge(z_ready, 1)
            for t in range(TT):
                o = bank[:, 4 + t, 0:2 * NF]
                if t % QT:
                    mm(o, ones[:, :], z5[:, t - 1, :], start=True, stop=False)
                mm(o, tri[:, :], z5[:, t, :], start=(t % QT == 0), stop=True).then_inc(sum_psum, 1)
            pe.wait_ge(o5_ready, 1)
            for t in range(TT):
                nc.tensor.transpose(bank[:, 0, t * P:(t + 1) * P], t5[:, t, 0:P], ident[:, :])
                nc.tensor.transpose(bank[:, 1, t * P:(t + 1) * P], t5[:, t, NF:NF + P], ident[:, :])
                last = nc.tensor.transpose(bank[0:1, 2, t * P:(t + 1) * P], t5[:, t, NF - 1:NF], ident[:, :])
            last.then_inc(o5T_psum, 1)
            pe.wait_ge(o5T_ready, 2)
            for t in range(TT):
                for c in range(DC):
                    mm(bank[:, 4 + t, 0:D], o5T[:, c, t * P:(t + 1) * P], idft[:, c, :], start=(c == 0), stop=False)
                mm(bank[:, 4 + t, 0:D], o5n[0:1, t * P:(t + 1) * P], idft_ny[0:1, :], start=False, stop=True)\
                    .then_inc(y5_psum, 1)

            pe.wait_ge(in_w6, 16 * N_W6)
            norm_T(5)
            for t in range(TT):
                for c in range(DC):
                    mm(bank[:, 2, t * E6:(t + 1) * E6], xnT[:, c, t * P:(t + 1) * P], sim6[:, c, :],
                       start=(c == 0), stop=(c == DC - 1))
            pe.wait_ge(sim_sq, 1)
            for c in range(DC):
                last = mm(bank[:, 3, 0:E6], ones[:, :], sim2[:, c, :], start=(c == 0), stop=(c == DC - 1))
            last.then_inc(logit6_psum, 1)
            for k in range(TT * E6 // 2):
                t, e = k // (E6 // 2), 2 * (k % (E6 // 2))
                if k >= 4:
                    pe.wait_ge(proj6_used, k - 3)
                for c in range(DC):
                    last = mm(bank[:, 4 + k % 4, 0:2 * QKV], xnT[:, c, t * P:(t + 1) * P],
                              w6[:, c, e:e + 2, :].rearrange("p a b -> p (a b)"), start=(c == 0), stop=(c == DC - 1))
                last.then_inc(proj6, 1)
            pe.wait_ge(qkv_ready, 1)
            for t in range(TT):
                nc.tensor.transpose(bank[0:HD6, 0, t * P:(t + 1) * P], qkv[:, t, 0:HD6], ident[:, :])
                last = nc.tensor.transpose(bank[0:HD6, 1, t * P:(t + 1) * P], qkv[:, t, HD6:2 * HD6], ident[:, :])
            last.then_inc(qk6_psum, 1)
            pe.wait_ge(qk6_ready, 1)
            for t in range(TT):
                w = S if t % QT else P
                b = t // QT
                mm(bank[:, 4 + t, 0:w], qT6[0:HD6, t * P:(t + 1) * P], kT6[0:HD6, b * S:b * S + w],
                   start=True, stop=True).then_inc(score6, 1)
            for t in range(TT):
                pe.wait_ge(norm6, t + 1)
                for k in range(t % QT + 1):
                    last = nc.tensor.transpose(bank[:, t % 2, k * P:(k + 1) * P], p6[:, t, k * P:(k + 1) * P], ident[:, :])
                last.then_inc(pT6_psum, 1)
                pe.wait_ge(pT6_ready, t + 1)
                for k in range(t % QT + 1):
                    last = mm(bank[:, 4 + t, 0:HD6], pT6[:, t, k, :], qkv[:, (t // QT) * QT + k, 2 * HD6:QKV],
                              start=(k == 0), stop=(k == t % QT))
                last.then_inc(att6, 1)
            for t in range(TT):
                pe.wait_ge(mix_ready, t + 1)
                if t >= 2:
                    pe.wait_ge(mixT_ready, t - 1)
                for j in range(8):
                    last = nc.tensor.transpose(bank[:, 2 * (t % 2) + j // 4, (j % 4) * P:(j % 4 + 1) * P],
                                               mixed[t % 2][:, j * P:(j + 1) * P], ident[:, :])
                last.then_inc(mixT_psum, 1)
                pe.wait_ge(mixT_ready, t + 1)
                for j in range(8):
                    last = mm(bank[:, 4 + t, 0:D], mixT[t % 2][:, j, :], wo6[:, j, :], start=(j == 0), stop=(j == 7))
                last.then_inc(y6_psum, 1)

        @block.vector
        def _(dve):
            v = nc.vector
            link = Link(dve, dve_link)

            def layer_norm(n):
                for t in range(TT):
                    last = v.bn_stats(stats[:, t, :], x[:, t, :])
                link(last)
                for t in range(TT):
                    last = v.bn_aggr(moments[:, t, :], stats[:, t, :])
                link(last)
                v.tensor_scalar(var_eps[:, :], moments[:, :, 1], EPS, None, ALU.add).then_inc(ln_var, 1)
                dve.wait_ge(ln_rstd, n + 1)
                for t in range(TT):
                    last = v.tensor_scalar(xn[:, t, :], x[:, t, :], moments[:, t, 0:1], rstd[:, t:t + 1],
                                           ALU.subtract, ALU.mult)
                last.then_inc(xn_ready, 1)
                dve.wait_ge(xn_ready, n + 1)

            def wide(r, n):
                return r.unsqueeze(2).broadcast_to([P, TT, n])

            def top2(vals, n, low):
                eq, rank, first, second = (pick[:, k, :, 0:n] for k in range(4))
                order = rev[:, 0:n].unsqueeze(1).broadcast_to([P, TT, n])
                for k, hot in enumerate((first, second)):
                    src = vals if k == 0 else eq
                    link(v.tensor_reduce(red[:, 0, :], src, AX.X, ALU.max))
                    link(v.tensor_tensor(rank, src, wide(red[:, 0, :], n), ALU.is_equal))
                    link(v.tensor_tensor(rank, rank, order, ALU.mult))
                    link(v.tensor_reduce(red[:, 1, :], rank, AX.X, ALU.max))
                    link(v.tensor_tensor(hot, rank, wide(red[:, 1, :], n), ALU.is_equal))
                    if k == 0:
                        link(v.tensor_scalar(eq, hot, low, None, ALU.mult))
                        link(v.tensor_tensor(eq, eq, vals, ALU.add))
                link(v.tensor_tensor(first, first, second, ALU.add))
                return first

            dve.wait_ge(in_const, 16 * N_CONST)
            v.tensor_copy(identb[:, :], ident[:, :]).then_inc(identb_ready, 1)
            v.memset(small[0:1, 0:1], 0.0).then_inc(x_added1, 1)
            v.memset(small[0:1, 1:2], 0.0).then_inc(pv_copied, 1)
            dve.wait_ge(in_x, 16)
            layer_norm(0)

            def turn1(b, i, first=False):
                for s in range(2):
                    dve.wait_ge(ctxT_ready, 2 * i + s + 1)
                    if not first:
                        dve.wait_ge(stored[s], 48 * i)
                    v.tensor_copy(split[s][:, 0, :, :], ctxT[s]).then_inc(high_ready, 1)
                    dve.wait_ge(high_ready, 2 * i + s + 1)
                    v.tensor_tensor(rest[s], ctxT[s], split[s][:, 0, :, :], ALU.subtract).then_inc(rest_ready, 1)
                dve.wait_ge(out1_pair, 4 * i + 4)
                dve.wait_ge(x_added1, i + 1)
                xs = x[:, b * QT:(b + 1) * QT, :]
                v.tensor_tensor(xs, xs, bank[:, 4:6, 0:D], ALU.add).then_inc(x_added1, 1)
            turn1(0, 0, True)
            with dve.Fori(1, TPB) as i:
                turn1(0, i)
            with dve.Fori(TPB, TURNS1) as i:
                turn1(1, i)
            dve.wait_ge(x_added1, TURNS1 + 1)

            layer_norm(1)
            dve.wait_ge(in_w2, 16 * N_W2)
            link(v.tensor_tensor(x[:, :, :], x[:, :, :], bo2.unsqueeze(1).broadcast_to([P, TT, D]), ALU.add))
            for n in range(TT * 2):
                t, c = n // 2, n % 2
                dve.wait_ge(v2_psum, n + 1)
                v.tensor_tensor(v2[:, t, c * 512:(c + 1) * 512], bank[:, n % 2, :], bv2[:, c * 512:(c + 1) * 512],
                                ALU.add).then_inc(v2_ready, 1)

            def max2(n):
                s = n % 2
                dve.wait_ge(score2, n + 1)
                link(v.tensor_reduce(sm2[s][:, 0, :], bank[:, 6 + s, :].rearrange("p (q k) -> p q k", q=QT), AX.X, ALU.max))
                v.tensor_scalar(sm2[s][:, 1, :], sm2[s][:, 0, :], -SCALE2, None, ALU.mult).then_inc(nmax2, 1)
            max2(0)
            for n in range(UNITS2):
                s = n % 2
                if n + 1 < UNITS2:
                    max2(n + 1)
                dve.wait_ge(exp2, n + 1)
                link(v.reciprocal(sm2[s][:, 3, :], sm2[s][:, 2, :]))
                v.tensor_tensor(p2[s], p2[s], sm2[s][:, 3, :].unsqueeze(2).broadcast_to([P, QT, S]), ALU.mult)\
                 .then_inc(norm2, 1)
                dve.wait_ge(pT2_psum, n + 1)
                v.tensor_copy(pT2[s].rearrange("p a b -> p (a b)"), bank[:, s, :]).then_inc(pT2_ready, 1)
            for t in range(TT):
                dve.wait_ge(y2_psum, t + 1)
                link(v.tensor_tensor(x[:, t, :], x[:, t, :], bank[:, 3 + t, 0:D], ALU.add))

            layer_norm(2)
            dve.wait_ge(logit3_psum, 1)
            logits = bank[:, 7, 0:TT * 16].rearrange("p (t e) -> p t e", t=TT)[:, :, 0:E3]
            link(v.tensor_reduce(red[:, 0, :], logits, AX.X, ALU.max))
            v.tensor_tensor(prob[:, :, 0:E3], logits, wide(red[:, 0, :], E3), ALU.subtract).then_inc(logit3, 1)

            def hiddens(k0):
                for f in range(FT):
                    m = P if f < FT - 1 else FLAST
                    dve.wait_ge(up_psum, k0 + f + 1)
                    dve.wait_ge(silu_ready, k0 + f + 1)
                    v.tensor_tensor(hid[f % 2][0:m, :], silu[f % 2][0:m, :], bank[0:m, 2 + f % 2, :], ALU.mult)\
                     .then_inc(hid_ready, 1)
            hiddens(0)
            dve.wait_ge(y3_psum, 1)
            v.tensor_tensor(x[:, :, :], x[:, :, :], bank[:, 4:8, 0:D], ALU.add).then_inc(y3_added, 1)
            dve.wait_ge(exp3, 1)
            pr = prob[:, :, 0:E3]
            link(v.tensor_reduce(red[:, 0, :], pr, AX.X, ALU.add))
            link(v.reciprocal(red[:, 1, :], red[:, 0, :]))
            link(v.tensor_tensor(pr, pr, wide(red[:, 1, :], E3), ALU.mult))
            chosen = top2(pr, E3, -4.0)
            w = weight[:, :, 0:E3]
            link(v.tensor_tensor(w, chosen, pr, ALU.mult))
            link(v.tensor_reduce(red[:, 0, :], w, AX.X, ALU.add))
            link(v.tensor_scalar(red[:, 0, :], red[:, 0, :], 1e-20, None, ALU.add))
            link(v.reciprocal(red[:, 1, :], red[:, 0, :]))
            link(v.tensor_tensor(w, w, wide(red[:, 1, :], E3), ALU.mult))
            with dve.Fori(0, E3 // 2) as i:
                for s in range(2):
                    n = 2 * i + s + 1
                    hiddens(n * FT)
                    dve.wait_ge(y3_psum, n + 1)
                    dve.wait_ge(y3_added, n)
                    for t in range(TT):
                        last = v.scalar_tensor_tensor(x[:, t, :], bank[:, 4 + t, 0:D],
                                                      weight[:, t, bass.ds(n - 1, 1)], x[:, t, :], ALU.mult, ALU.add)
                    last.then_inc(y3_added, 1)
            dve.wait_ge(y3_added, E3 + 1)

            layer_norm(3)
            xq = xn[:, :, :].rearrange("p t (h d) -> p t h d", d=DH4)
            rest_q = q_rest.rearrange("p t (h d) -> p t h d", d=DH4)

            def term(n):
                return q_rows[:, :, :, n * DH4:(n + 1) * DH4]
            link(v.tensor_copy(term(0), xq))
            link(v.tensor_tensor(rest_q, xq, term(0), ALU.subtract))
            link(v.tensor_copy(term(1), rest_q))
            link(v.tensor_tensor(term(2), rest_q, term(1), ALU.subtract))
            v.tensor_copy(term(3), term(0))
            v.tensor_copy(term(4), term(1))
            v.tensor_copy(term(5), term(0)).then_inc(q_rows_ready, 1)
            dve.wait_ge(qT_ready, TT * 2)

            def take_max(k, m):
                q, c = m % 2, m // 2
                dve.wait_ge(max_psum, k + 1)
                v.memset(small[0:1, 1 + q:2 + q], 0.0)
                v.tensor_tensor_reduce(out=junk[q], in0=bank[:, 4 + q, :], in1=maskN[:, q, c * CH:(c + 1) * CH], scale=1.0,
                                       scalar=-3.0e38, op0=ALU.add, op1=ALU.max, accum_out=cmax[:, q, c:c + 1])\
                 .then_inc(max_taken, 1)

            def negmax_parts(u):
                dve.wait_ge(max_taken, u * MAXES + MAXES)
                link(v.tensor_reduce(negmax[:, 0, :], cmax, AX.X, ALU.max, negate=True))
                link(v.tensor_copy(negparts[:, :, 0], negmax[:, 0, :]))
                link(v.tensor_tensor(negmax[:, 1, :], negmax[:, 0, :], negparts[:, :, 0], ALU.subtract))
                link(v.tensor_copy(negparts[:, :, 1], negmax[:, 1, :]))
                v.tensor_tensor(negparts[:, :, 2], negmax[:, 1, :], negparts[:, :, 1], ALU.subtract)\
                 .then_inc(negmax_ready, 1)

            def negmax_row(u):
                dve.wait_ge(negT_psum, u + 1)
                v.tensor_copy(qT4[KROWS:KALL, bass.ds(u, 1), :].rearrange("p o q -> p (o q)"),
                              bf16_bank(7)[KROWS:KALL, 0:S]).then_inc(negT_ready, 1)

            def unit(u, more):
                if more:
                    for m in range(MAXES):
                        take_max(u * MAXES + MAXES + m, m)
                    negmax_parts(u + 1)
                    negmax_row(u + 1)
                dve.wait_ge(pv_psum, u + 1)
                v.tensor_copy(pv_sb, bank[:, 6, 0:S]).then_inc(pv_copied, 1)
                dve.wait_ge(oT_psum, u + 1)
                parts = bank[:, 7, 256:512].rearrange("p (q j d) -> p q d j", q=QT, j=4)[:, :, 0:DH4 + 1, :]
                link(v.tensor_reduce(osum, parts, AX.X, ALU.add))
                link(v.reciprocal(orec, osum[:, :, DH4]))
                v.tensor_tensor(o4[:, :, bass.ds(u * DH4, DH4)], osum[:, :, 0:DH4],
                                orec.unsqueeze(2).broadcast_to([P, QT, DH4]), ALU.mult).then_inc(o4_unit, 1)

            for m in range(MAXES):
                take_max(m, m)
            negmax_parts(0)
            negmax_row(0)
            with dve.Fori(0, U4 - 1) as i:
                link.loop(i, 6)
                unit(i, True)
            link.end(U4 - 1)
            unit(U4 - 1, False)
            dve.wait_ge(o4_unit, U4)
            dve.wait_ge(in_wout, 32)
            v.tensor_tensor(x[:, :, :], x[:, :, :], bo4.unsqueeze(1).broadcast_to([P, TT, D]), ALU.add)\
             .then_inc(o4_ready, 1)
            dve.wait_ge(o4_ready, 1)
            dve.wait_ge(y4_psum, TT)
            link(v.tensor_tensor(x[:, :, :], x[:, :, :], bank[:, 0:4, 0:D], ALU.add))

            layer_norm(4)
            for n in range(3):
                dve.wait_ge(mag_ready, n)
                dve.wait_ge(spec_ready, 2 * n + 2)
                link(v.tensor_tensor(mag, spec[:, n, :, :], spec[:, n, :, :], ALU.mult))
                v.tensor_tensor(magr[:, n, :, :], mag[:, :, 0:NF], mag[:, :, NF:2 * NF], ALU.add).then_inc(mag_ready, 1)
            for n in range(3):
                m = magr[:, n, :, :]
                dve.wait_ge(root_ready, n + 1)
                link(v.tensor_scalar(m, m, 1e-8, None, ALU.add))
                link(v.reciprocal(m, m))
                for c in range(2):
                    part = spec[:, n, :, c * NF:(c + 1) * NF]
                    last = v.tensor_tensor(part, part, m, ALU.mult)
                link(last)
            re, im = slice(0, NF), slice(NF, 2 * NF)

            def product(o, l, r, tmp, sign):
                add, sub = (ALU.add, ALU.subtract) if sign > 0 else (ALU.subtract, ALU.add)
                v.tensor_tensor(o[:, :, re], l[:, :, re], r[:, :, re], ALU.mult)
                link(v.tensor_tensor(tmp[:, :, re], l[:, :, im], r[:, :, im], ALU.mult))
                link(v.tensor_tensor(o[:, :, re], o[:, :, re], tmp[:, :, re], sub))
                v.tensor_tensor(o[:, :, im], l[:, :, im], r[:, :, re], ALU.mult)
                link(v.tensor_tensor(tmp[:, :, im], l[:, :, re], r[:, :, im], ALU.mult))
                return v.tensor_tensor(o[:, :, im], o[:, :, im], tmp[:, :, im], add)
            product(z5, spec[:, 0, :, :], spec[:, 1, :, :], mag, 1).then_inc(z_ready, 1)
            dve.wait_ge(sum_psum, TT)
            product(t5, bank[:, 4:8, 0:2 * NF], spec[:, 2, :, :], mag, -1).then_inc(o5_ready, 1)
            dve.wait_ge(y5_psum, TT)
            link(v.tensor_tensor(x[:, :, :], x[:, :, :], bank[:, 4:8, 0:D], ALU.add))

            layer_norm(5)
            dve.wait_ge(in_w6, 16 * N_W6)
            v.tensor_tensor(sim2, sim6, sim6, ALU.mult).then_inc(sim_sq, 1)
            v.tensor_scalar(col6[:, 1, :], gates6, 1.0, None, ALU.mult).then_inc(gate_arg, 1)
            link(v.tensor_tensor(sq6, xn[:, :, :], xn[:, :, :], ALU.mult))
            v.tensor_reduce(square6[:, 0:TT], sq6, AX.X, ALU.add)
            dve.wait_ge(logit6_psum, 1)
            v.tensor_copy(square6[:, TT:TT + E6], bank[:, 3, 0:E6]).then_inc(pow_arg, 1)
            dve.wait_ge(pow_ready, 1)
            link(v.tensor_scalar(root6[:, :], root6[:, :], 1e-12, None, ALU.max))
            link(v.reciprocal(root6[:, :], root6[:, :]))
            dve.wait_ge(gate_exp, 1)
            link(v.tensor_scalar(col6[:, 2, :], col6[:, 0, :], 1.0, None, ALU.add))
            link(v.reciprocal(col6[:, 3, :], col6[:, 2, :]))
            lg = bank[:, 2, 0:TT * E6].rearrange("p (t e) -> p t e", t=TT)

            def row(r):
                return r.unsqueeze(1).broadcast_to([P, TT, E6])
            link(v.tensor_tensor(logit6, lg, wide(root6[:, 0:TT], E6), ALU.mult))
            link(v.tensor_tensor(logit6, logit6, row(root6[:, TT:TT + E6]), ALU.mult))
            link(v.tensor_tensor(logit6, logit6, row(col6[:, 3, :]), ALU.subtract))
            fallback = top2(logit6, E6, -1.0e30)
            active, gated, used = (pick[:, k, :, :] for k in (1, 2, 4))
            link(v.tensor_scalar(active, logit6, 0.0, None, ALU.is_gt))
            link(v.tensor_reduce(red[:, 2, :], active, AX.X, ALU.max))
            link(v.tensor_scalar(red[:, 3, :], red[:, 2, :], 0.0, None, ALU.is_equal))
            link(v.tensor_tensor(used, fallback, wide(red[:, 3, :], E6), ALU.mult))
            link(v.tensor_tensor(used, used, active, ALU.add))
            link(v.tensor_scalar(gated, logit6, 0.0, None, ALU.max))
            link(v.tensor_reduce(red[:, 2, :], gated, AX.X, ALU.max))
            v.tensor_tensor(prob[:, :, :], gated, wide(red[:, 2, :], E6), ALU.subtract).then_inc(exp6w_arg, 1)
            dve.wait_ge(exp6w, 1)
            link(v.tensor_tensor(weight[:, :, :], prob[:, :, :], used, ALU.mult))
            link(v.tensor_reduce(red[:, 2, :], weight[:, :, :], AX.X, ALU.add))
            link(v.reciprocal(red[:, 3, :], red[:, 2, :]))
            link(v.tensor_tensor(weight[:, :, :], weight[:, :, :], wide(red[:, 3, :], E6), ALU.mult))
            for k in range(TT * E6 // 2):
                t, e = k // (E6 // 2), 2 * (k % (E6 // 2))
                dve.wait_ge(proj6, k + 1)
                for j in range(2):
                    src = bank[:, 4 + k % 4, j * QKV:(j + 1) * QKV]
                    wt = weight[:, t, e + j:e + j + 1]
                    if e + j == 0:
                        link(v.tensor_scalar(qkv[:, t, :], src, wt, None, ALU.mult))
                    elif j == 0:
                        link(v.scalar_tensor_tensor(qkv[:, t, :], src, wt, qkv[:, t, :], ALU.mult, ALU.add))
                    else:
                        v.scalar_tensor_tensor(qkv[:, t, :], src, wt, qkv[:, t, :], ALU.mult, ALU.add)\
                         .then_inc(proj6_used, 1)
                        dve.wait_ge(proj6_used, k + 1)
            v.tensor_copy(small[:, 0:1], red[:, 0, 0:1]).then_inc(qkv_ready, 1)
            for t in range(TT):
                dve.wait_ge(score6, t + 1)
                lo = P if t % QT else 0
                if lo:
                    v.tensor_scalar(p6[:, t, 0:P], bank[:, 4 + t, 0:P], SCALE6, None, ALU.mult)
                link(v.scalar_tensor_tensor(p6[:, t, lo:lo + P], bank[:, 4 + t, lo:lo + P], SCALE6, causal[:, :],
                                            ALU.mult, ALU.add))
                v.tensor_reduce(row6[:, 2, t:t + 1], p6[:, t, 0:lo + P], AX.X, ALU.max, negate=True).then_inc(nmax6, 1)
            for t in range(TT):
                w = S if t % QT else P
                dve.wait_ge(exp6, t + 1)
                link(v.reciprocal(row6[:, 0, t:t + 1], row6[:, 3, t:t + 1]))
                v.tensor_scalar(p6[:, t, 0:w], p6[:, t, 0:w], row6[:, 0, t:t + 1], None, ALU.mult).then_inc(norm6, 1)
                dve.wait_ge(pT6_psum, t + 1)
                v.tensor_copy(pT6[:, t, :, :].rearrange("p a b -> p (a b)")[:, 0:w], bank[:, t % 2, 0:w])\
                 .then_inc(pT6_ready, 1)
            for t in range(TT):
                dve.wait_ge(att6, t + 1)
                if t >= 2:
                    dve.wait_ge(mixT_psum, t - 1)
                v.tensor_tensor(mixed[t % 2].rearrange("p (e d) -> p e d", d=HD6),
                                bank[:, 4 + t, 0:HD6].unsqueeze(1).broadcast_to([P, E6, HD6]),
                                weight[:, t, :].unsqueeze(2).broadcast_to([P, E6, HD6]), ALU.mult)\
                 .then_inc(mix_ready, 1)
            for t in range(TT):
                dve.wait_ge(y6_psum, t + 1)
                last = v.tensor_tensor(x[:, t, :], x[:, t, :], bank[:, 4 + t, 0:D], ALU.add)
            last.then_inc(x_final, 1)


def constants():
    n, f = np.arange(D)[:, None], np.arange(NF)[None, :]
    angle = 2 * np.pi * ((n * f) % D) / D
    share = np.where((f == 0) | (f == NF - 1), 1.0, 2.0) / D
    inverse = np.concatenate([(share * np.cos(angle)).T[:NF - 1], (-share * np.sin(angle)).T[:NF - 1],
                              (share * np.cos(angle)).T[NF - 1:]])
    i = np.arange(P)
    return {
        "c_ident": np.eye(P, dtype=np.float32),
        "c_tri": (i[:, None] <= i[None, :]).astype(np.float32),
        "c_causal": np.where(i[:, None] >= i[None, :], 0.0, -1e30).astype(np.float32),
        "c_rev": np.arange(16, 0, -1).astype(np.float32),
        "c_dft": np.concatenate([np.cos(angle), -np.sin(angle)], axis=1).astype(np.float32),
        "c_idft": inverse.astype(np.float32),
    }


def kernel(**inputs):
    import concourse.bacc as bacc
    from concourse.bass_utils import run_bass_kernel_spmd

    nc = bacc.Bacc("TRN2", target_bir_lowering=False, num_devices=1)
    arrays, views = {}, {}
    for name, value in list(inputs.items()) + list(constants().items()):
        array = np.ascontiguousarray(value)
        arrays[f"in_{name}"] = array
        views[name] = nc.dram_tensor(f"in_{name}", array.shape, mybir.dt.from_np(array.dtype),
                                     kind="ExternalInput").ap()
    out = nc.dram_tensor("out", (B, S, D), F32, kind="ExternalOutput").ap()
    build(nc, views, out)
    r = run_bass_kernel_spmd(nc, [arrays], core_ids=[0])
    return r.results[0]["out"]
```

```python
from contextlib import ExitStack

import numpy as np

import concourse.bass as bass
from concourse import mybir

ALU = mybir.AluOpType
ACT = mybir.ActivationFunctionType
AX = mybir.AxisListType
F32 = mybir.dt.float32
BF16 = mybir.dt.bfloat16
I32 = mybir.dt.int32

P = 128
B, S, D = 2, 256, 256
T = B * S
TT = T // P
DC = D // P
CTX = 4096
QT = S // P

CH = 512
NCH = B * CTX // CH
SLOTS1 = 4
TURNS1 = NCH // SLOTS1
TPB = TURNS1 // B

H2, DK, DCQ, DR = 8, 128, 32, 32
UNITS2 = H2 * B

E3, F3, TOP = 8, 688, 2
FT = (F3 + P - 1) // P
FLAST = F3 - (FT - 1) * P

H4, DH4 = 16, 16
U4 = B * H4
TERMS = 6
KROWS = TERMS * DH4
KALL = KROWS + 3
GROUPS = 8
KT4 = CTX // P
RING = 4
MAXES = 2 * GROUPS
AHEAD = 4
MASKED = -float((np.float32(1e20).view(np.uint32) & np.uint32(0xFFFF0000)).view(np.float32))
K_PARTS = (0, 0, 0, 1, 1, 2)
Q_PARTS = (0, 1, 2, 0, 1, 0)

NF = D // 2 + 1

E6, HD6 = 16, 64
QKV = 3 * HD6
DEEP6 = (4, 5, 6, 7, 3, 0, 1)

N_CONST = 4
N_W2 = 15
N_W5 = 9
N_W6 = 7
EPS = 1e-5
SCALE2 = float((DK + DR) ** -0.5)
SCALE4 = float(D) ** -0.5
SCALE6 = float(HD6) ** -0.5


class Arena:

    def __init__(self, tensor):
        self.t, self.at = tensor, 0

    def take(self, shape, dt=F32, parts=(0, P), at=None):
        if at is not None:
            self.at = at
        size = 2 if dt == BF16 else 4
        n = int(np.prod(shape)) * size
        n = (n + 3) // 4 * 4
        v = self.t[parts[0]:parts[1], self.at // 4:(self.at + n) // 4]
        self.at += n
        assert self.at <= self.t.shape[1] * 4, (self.at, self.t.shape)
        if dt != F32:
            v = v.bitcast(dt)
        if len(shape) == 1:
            return v
        names = "abcd"[:len(shape)]
        return v.rearrange(f"p ({' '.join(names)}) -> p {' '.join(names)}",
                           **dict(zip(names[1:], shape[1:])))


class Link:

    def __init__(self, eng, sem):
        self.eng, self.sem, self.base, self.k = eng, sem, 0, 0

    def __call__(self, ins):
        self.k += 1
        ins.then_inc(self.sem, 1)
        self.eng.wait_ge(self.sem, self.base + self.k)

    def loop(self, i, per):
        self.start, self.per = self.base + self.k, per
        self.base, self.k = self.start + i * per, 0

    def end(self, turns):
        assert self.k == self.per, (self.k, self.per)
        self.base, self.k = self.start + turns * self.per, 0


def build(nc, a, out):
    ctx = ExitStack()
    with ctx:
        def sb(name, shape, dt=F32):
            return ctx.enter_context(nc.sbuf_tensor(name, shape, dt))

        def sem(name):
            return ctx.enter_context(nc.semaphore(name))

        keys_dram = nc.dram_tensor("keys_split", (3, B * D, CTX), BF16, kind="Internal").ap()

        bank = ctx.enter_context(nc.psum_tensor("bank", [P, 8, 512], F32))

        x = sb("x", [P, TT, D])
        xn = sb("xn", [P, TT, D])
        xnT = sb("xnT", [P, DC, T])
        ident = sb("ident", [P, P])
        identb = sb("identb", [P, P], BF16)
        ones = sb("ones", [P, P])
        tri = sb("tri", [P, P])
        causal = sb("causal", [P, P])
        rev = sb("rev", [P, 16])
        stats = sb("stats", [P, TT, 6])
        moments = sb("moments", [P, TT, 2])
        var_eps = sb("var_eps", [P, TT])
        rstd = sb("rstd", [P, TT])
        minus_half = sb("minus_half", [P, TT])
        gate3 = sb("gate3", [P, DC, E3])
        bdown = sb("bdown", [96, 1])
        bq2 = sb("bq2", [P, H2])
        bk2 = sb("bk2", [P, H2])
        bqr2 = sb("bqr2", [96, H2])
        prob = sb("prob", [P, TT, 16])
        pick = sb("pick", [P, 6, TT, 16])
        red = sb("red", [P, 6, TT])
        weight = sb("weight", [P, TT, 16])
        small = sb("small", [P, 8])
        square6 = sb("square6", [P, TT + E6])
        root6 = sb("root6", [P, TT + E6])
        half = sb("half", [P, TT + E6])
        woutT = sb("woutT", [P, DC, D])

        A1 = Arena(sb("region1", [P, 16384]))
        A2 = Arena(sb("region2", [P, 12288]))
        A3 = Arena(sb("region3", [P, 16384]))

        ctx_in = [A2.take([4, D], at=0 if s == 0 else None) for s in range(SLOTS1)]
        ctxT = [A2.take([DC, CH]) for s in range(2)]
        geluT = [A2.take([2, S]) for s in range(2)]
        split = [A2.take([3, DC, CH], BF16) for s in range(2)]
        rest = [A2.take([DC, CH]) for s in range(2)]
        maskN = A3.take([QT, CTX], BF16, at=0)
        maskT = A3.take([KT4, S], BF16)
        mask_raw = A3.take([QT, CTX], I32)
        v2 = A1.take([TT, H2 * DK], at=0)
        oT2 = A1.take([H2, T])
        up = A1.take([2, H2 * DK])
        bv2 = A1.take([H2 * DK])
        bo2 = A1.take([D])
        wdown = A1.take([DC, 96])
        downT = A1.take([T])
        qT2 = [A1.take([T]) for s in range(2)]
        kT2 = [A1.take([T]) for s in range(2)]
        wo2 = A3.take([H2, D], at=32768)
        qrT2 = [A3.take([T]) for s in range(2)]
        p2 = [A3.take([QT, S]) for s in range(2)]
        pT2 = [A3.take([2, S]) for s in range(2)]
        sm2 = [A3.take([5, QT]) for s in range(2)]
        w3 = []
        A2.at = 0
        for s in range(2):
            w3.append((A2.take([DC, F3]), A2.take([DC, F3]), A2.take([FT, D])))
        silu = [A2.take([T]) for s in range(2)]
        hid = [A2.take([T]) for s in range(2)]
        ctx_nat = A1.take([KT4, B * D], at=0)
        qT4 = A3.take([U4, S], BF16, at=32768)
        slab = [A3.take([CTX], BF16), A3.take([CTX], BF16), A2.take([CTX], BF16, at=0), A2.take([CTX], BF16)]
        vaug = [A2.take([KT4, 32]) for s in range(2)]
        at = A2.at
        q_rows = A2.take([TT, H4, KROWS], BF16)
        q_rest = A2.take([TT, D])
        prob4 = [A2.take([4, S], at=at if s == 0 else None) for s in range(2)]
        junk = [A2.take([CH], BF16) for q in range(QT)]
        pv_sb = A2.take([S])
        o4 = A2.take([QT, B * D])
        o4T = A2.take([DC, T])
        bo4 = A2.take([D])
        cmax = [A2.take([QT, GROUPS]) for s in range(2)]
        negmax = A2.take([2, QT])
        negparts = A2.take([QT, 4], BF16)
        osum = A2.take([QT, 17])
        orec = A2.take([QT])
        wout = sb("wout", [P, DC, D])
        w5 = A3.take([3, DC, D], at=0)
        b5 = A3.take([3, DC])
        dft = A3.take([DC, 2 * NF])
        idft = A3.take([DC, D])
        idft_ny = A3.take([D])
        fold = A3.take([3, DC, 2 * NF])
        brow = A3.take([3, 2 * NF])
        spec = A3.take([3, TT, 2 * NF])
        mag = A3.take([TT, 2 * NF])
        magr = A3.take([3, TT, NF])
        z5 = A3.take([TT, 2 * NF])
        t5 = A3.take([TT, 2 * NF])
        o5T = A3.take([DC, T])
        o5n = A3.take([T])
        w6 = A1.take([DC, E6, QKV], at=0)
        wo6 = A1.take([E6 * HD6 // P, D])
        sim6 = A1.take([DC, E6])
        sim2 = A1.take([DC, E6])
        gates6 = A1.take([E6])
        col6 = A1.take([4, E6])
        row6 = A1.take([4, TT])
        sq6 = A1.take([TT, D])
        logit6 = A1.take([TT, E6])
        qkv = A1.take([TT, QKV])
        qT6 = A1.take([T])
        kT6 = A1.take([T])
        p6 = A1.take([TT, S])
        pT6 = A1.take([TT, 2, P])
        mixed = [A1.take([E6 * HD6]) for s in range(2)]
        mixT = [A2.take([E6 * HD6 // P, P], at=0 if s == 0 else None) for s in range(2)]

        in_gate3, in_gate6 = sem("in_gate3"), sem("in_gate6")
        in_x, in_const, in_mask = sem("in_x"), sem("in_const"), sem("in_mask")
        dve_link, pool_link, act_link = sem("dve_link"), sem("pool_link"), sem("act_link")
        setup, identb_ready = sem("setup"), sem("identb_ready")
        ln_var, ln_rstd, xn_ready, xnT_psum, xnT_ready = (
            sem("ln_var"), sem("ln_rstd"), sem("xn_ready"), sem("xnT_psum"), sem("xnT_ready"))
        mask_ready, maskT_psum, maskT_ready = sem("mask_ready"), sem("maskT_psum"), sem("maskT_ready")
        ctx_loaded = [sem(f"ctx_loaded{s}") for s in range(SLOTS1)]
        ctxT_psum, ctxT_ready = sem("ctxT_psum"), sem("ctxT_ready")
        h1_ready, gelu_ready, out1_pair, x_added1 = (
            sem("h1_ready"), sem("gelu_ready"), sem("out1_pair"), sem("x_added1"))
        rest_ready, stored = sem("rest_ready"), [sem(f"stored{s}") for s in range(2)]
        in_w2, in_wo2 = sem("in_w2"), sem("in_wo2")
        down_psum, down_ready = sem("down_psum"), sem("down_ready")
        v2_psum, v2_ready = sem("v2_psum"), sem("v2_ready")
        proj2_psum, proj2_ready = sem("proj2_psum"), sem("proj2_ready")
        score2, nmax2, exp2, norm2 = sem("score2"), sem("nmax2"), sem("exp2"), sem("norm2")
        pT2_psum, pT2_ready = sem("pT2_psum"), sem("pT2_ready")
        o2_psum, o2_ready, y2_psum = sem("o2_psum"), sem("o2_ready"), sem("y2_psum")
        high_ready, mid_ready, low_ready = sem("high_ready"), sem("mid_ready"), sem("low_ready")
        v_blank = sem("v_blank")
        logit3_psum, slab_ones, o4_unit = sem("logit3_psum"), sem("slab_ones"), sem("o4_unit")
        in_w3 = [sem(f"in_w3_{s}") for s in range(2)]
        logit3, exp3 = sem("logit3"), sem("exp3")
        gate_psum, up_psum, silu_ready, hid_ready, hid_used = (
            sem("gate_psum"), sem("up_psum"), sem("silu_ready"), sem("hid_ready"), sem("hid_used"))
        y3_psum, y3_added = sem("y3_psum"), sem("y3_added")
        in_ctx, in_wout = sem("in_ctx"), sem("in_wout")
        q_rows_ready, qT_psum, qT_ready = sem("q_rows_ready"), sem("qT_psum"), sem("qT_ready")
        slab_loaded = [sem(f"slab_loaded{s}") for s in range(RING)]
        v_ready = sem("v_ready")
        score4, exp4_ready = sem("score4"), sem("exp4_ready")
        max_psum, max_taken, negmax_ready, negT_psum, negT_ready = (
            sem("max_psum"), sem("max_taken"), sem("negmax_ready"), sem("negT_psum"), sem("negT_ready"))
        pv_psum, pv_copied, oT_psum, oT_used = (
            sem("pv_psum"), sem("pv_copied"), sem("oT_psum"), sem("oT_used"))
        o4_ready, o4T_psum, o4T_ready, y4_psum = (
            sem("o4_ready"), sem("o4T_psum"), sem("o4T_ready"), sem("y4_psum"))
        wout_psum, wout_ready = sem("wout_psum"), sem("wout_ready")
        in_w5, fold_psum, fold_ready = sem("in_w5"), sem("fold_psum"), sem("fold_ready")
        spec_psum, spec_ready, mag_ready, root_ready = (
            sem("spec_psum"), sem("spec_ready"), sem("mag_ready"), sem("root_ready"))
        z_ready, sum_psum, o5_ready, o5T_psum, o5T_ready, y5_psum = (
            sem("z_ready"), sem("sum_psum"), sem("o5_ready"), sem("o5T_psum"), sem("o5T_ready"), sem("y5_psum"))
        in_w6, sim_sq, logit6_psum, norm6_psum, gate_exp = (
            sem("in_w6"), sem("sim_sq"), sem("logit6_psum"), sem("norm6_psum"), sem("gate_exp"))
        pow_arg, pow_ready, exp6w_arg, exp6w = sem("pow_arg"), sem("pow_ready"), sem("exp6w_arg"), sem("exp6w")
        proj6, proj6_used, qk6_psum, qk6_ready = sem("proj6"), sem("proj6_used"), sem("qk6_psum"), sem("qk6_ready")
        qkv_ready, score6, nmax6, exp6, norm6 = (
            sem("qkv_ready"), sem("score6"), sem("nmax6"), sem("exp6"), sem("norm6"))
        pT6_psum, pT6_ready, att6 = sem("pT6_psum"), sem("pT6_ready"), sem("att6")
        mix_ready, mixT_psum, mixT_ready, y6_psum = (
            sem("mix_ready"), sem("mixT_psum"), sem("mixT_ready"), sem("y6_psum"))
        x_final, out_stored = sem("x_final"), sem("out_stored")

        block = ctx.enter_context(nc.Block())

        def bf16_bank(n):
            return bank[:, n, :].bitcast(BF16)

        def cols(t, start, n=P):
            return slice(start, start + n)

        @block.sync
        def _(sp):
            sp.dma_start(x[:, :, :], a["x"].rearrange("b (t p) d -> p (b t) d", p=P)).then_inc(in_x, 16)
            for dst, name in ((ident, "c_ident"), (tri, "c_tri"), (causal, "c_causal")):
                sp.dma_start(dst[:, :], a[name]).then_inc(in_const, 16)
            sp.dma_start(rev[:, :], a["c_rev"].partition_broadcast(P)).then_inc(in_const, 16)

            chunks = a["ctx_1024"].rearrange("b (c t p) d -> (b c) p t d", t=4, p=P)

            def load_chunk(s, c):
                sp.dma_start(ctx_in[s], chunks[bass.ds(c, 1)].rearrange("o p t d -> p (o t) d"))\
                  .then_inc(ctx_loaded[s], 16)
            for s in range(SLOTS1):
                load_chunk(s, s)
            sp.dma_start(mask_raw, a["mask_1x1xSxS2_ik0"].rearrange("a b (t p) k -> p (a b t) k", p=P))\
              .then_inc(in_mask, 16)
            for c in range(DC):
                sp.dma_start(gate3[:, c, :], a["L0_ffn_gate_w"][:, c * P:(c + 1) * P].rearrange("e p -> p e"),
                             allow_slow_non_contiguous=True)\
                  .then_inc(in_gate3, 16)
            for n, name in enumerate(("DQ", "DKV", "KR")):
                sp.dma_start(bdown[32 * n:32 * n + 32, :], a["L0_attn_b_" + name].rearrange("(p o) -> p o", o=1),
                             allow_slow_non_contiguous=True)\
                  .then_inc(in_w2, 16)
                sp.dma_start(wdown[:, :, 32 * n:32 * n + 32],
                             a["L0_attn_W_" + name].rearrange("(c p) n -> p c n", p=P)).then_inc(in_w2, 16)
            sp.dma_start(bq2[:, :], a["L0_attn_b_UQ"].rearrange("(h p) -> p h", p=P), allow_slow_non_contiguous=True).then_inc(in_w2, 16)
            sp.dma_start(bk2[:, :], a["L0_attn_b_UK"].rearrange("(h p) -> p h", p=P), allow_slow_non_contiguous=True).then_inc(in_w2, 16)
            sp.dma_start(bqr2[64:96, :], a["L0_attn_b_QR"].rearrange("(h p) -> p h", p=DR), allow_slow_non_contiguous=True).then_inc(in_w2, 16)
            sp.dma_start(up[0:32, 0, :], a["L0_attn_W_UQ"]).then_inc(in_w2, 16)
            sp.dma_start(up[0:32, 1, 0:H2 * DR], a["L0_attn_W_QR"]).then_inc(in_w2, 16)
            sp.dma_start(up[32:64, 0, :], a["L0_attn_W_UK"]).then_inc(in_w2, 16)
            sp.dma_start(up[32:64, 1, :], a["L0_attn_W_UV"]).then_inc(in_w2, 16)
            sp.dma_start(bv2, a["L0_attn_b_UV"].partition_broadcast(P)).then_inc(in_w2, 16)
            sp.dma_start(bo2, a["L0_attn_b_O"].partition_broadcast(P)).then_inc(in_w2, 16)
            sp.dma_start(wout[:, :, :], a["L1_xattn_w_out"].rearrange("(c p) n -> p c n", p=P)).then_inc(in_wout, 16)
            with sp.Fori(0, TURNS1 - 1) as i:
                for s in range(SLOTS1):
                    sp.wait_ge(out1_pair, 2 * SLOTS1 * i + 2 * s + 2)
                    load_chunk(s, SLOTS1 * i + s + SLOTS1)

            sp.wait_ge(mask_ready, QT)
            sp.dma_start(wo2, a["L0_attn_W_O"].rearrange("(h p) n -> p h n", p=P)).then_inc(in_wo2, 16)

            def load_expert(s, gate, upw, down):
                g, u, d = w3[s]
                sp.dma_start(g, gate.rearrange("(c p) n -> p c n", p=P)).then_inc(in_w3[s], 16)
                sp.dma_start(u, upw.rearrange("(c p) n -> p c n", p=P)).then_inc(in_w3[s], 16)
                sp.dma_start(d[:, 0:FT - 1, :], down[0:(FT - 1) * P, :].rearrange("(c p) n -> p c n", p=P))\
                  .then_inc(in_w3[s], 16)
                sp.dma_start(d[0:FLAST, FT - 1, :], down[(FT - 1) * P:F3, :]).then_inc(in_w3[s], 16)

            def routed(e):
                return [a[n][bass.ds(e, 1)].rearrange("o a b -> (o a) b")
                        for n in ("L0_ffn_we_gate", "L0_ffn_we_up", "L0_ffn_we_down")]
            for s in range(2):
                sp.wait_ge(stored[s], 48 * NCH // 2)
            sp.wait_ge(x_added1, TURNS1 + 1)
            load_expert(0, a["L0_ffn_sw_gate"], a["L0_ffn_sw_up"], a["L0_ffn_sw_down"])
            load_expert(1, *routed(0))
            sp.wait_ge(xn_ready, 3)
            for b in range(B):
                sp.dma_start(ctx_nat[:, :, b * D:(b + 1) * D],
                             a["ctx_1024"][b].rearrange("(t p) d -> p t d", p=P)).then_inc(in_ctx, 16)

            def load_slab(s, u):
                for n, part in enumerate(K_PARTS):
                    sp.dma_start(slab[s][n * DH4:(n + 1) * DH4, :],
                                 keys_dram[part, bass.ds(u * DH4, DH4), :]).then_inc(slab_loaded[s], 16)
            for s in range(2):
                load_slab(s, s)
            with sp.Fori(0, E3 // 2 - 1) as i:
                sp.wait_ge(y3_psum, 2 * i + 1)
                load_expert(0, *routed(2 * i + 1))
                sp.wait_ge(y3_psum, 2 * i + 2)
                load_expert(1, *routed(2 * i + 2))
            sp.wait_ge(y3_psum, E3 - 1)
            load_expert(0, *routed(E3 - 1))

            sp.wait_ge(xn_ready, 4)
            sp.dma_start(bo4, a["L1_xattn_b_out"].partition_broadcast(P)).then_inc(in_wout, 16)
            for s in range(2, RING):
                load_slab(s, s)
            with sp.Fori(0, U4 // RING - 1) as i:
                for s in range(RING):
                    sp.wait_ge(score4, GROUPS * RING * i + GROUPS * (s + 1))
                    load_slab(s, RING * i + s + RING)
            sp.wait_ge(v_ready, U4)
            sp.dma_start(sim6, a["L1_ffn_sim_matrix"].rearrange("(c p) e -> p c e", p=P)).then_inc(in_gate6, 16)
            sp.dma_start(gates6, a["L1_ffn_gates"].partition_broadcast(P)).then_inc(in_gate6, 16)
            sp.wait_ge(score4, GROUPS * U4)
            sp.wait_ge(max_taken, MAXES * U4)
            for n, name in enumerate("kvq"):
                sp.dma_start(w5[:, n, :, :], a["L1_attn_W" + name].rearrange("(c p) n -> p c n", p=P)).then_inc(in_w5, 16)
                sp.dma_start(b5[:, n, :], a["L1_attn_b" + name].rearrange("(c p) -> p c", p=P), allow_slow_non_contiguous=True).then_inc(in_w5, 16)
            sp.dma_start(dft, a["c_dft"].rearrange("(c p) n -> p c n", p=P)).then_inc(in_w5, 16)
            sp.dma_start(idft, a["c_idft"][0:D, :].rearrange("(c p) n -> p c n", p=P)).then_inc(in_w5, 16)
            sp.dma_start(idft_ny[0:1, :], a["c_idft"][D:D + 1, :]).then_inc(in_w5, 16)
            for n, name in enumerate("qkv"):
                for c in range(DC):
                    sp.dma_start(w6[:, c, :, n * HD6:(n + 1) * HD6],
                                 a[f"L1_ffn_{name}_proj"][:, c * P:(c + 1) * P, :].rearrange("e p d -> p e d"))\
                      .then_inc(in_w6, 16)
            sp.dma_start(wo6, a["L1_ffn_o_proj"].rearrange("e d n -> (e d) n").rearrange("(j p) n -> p j n", p=P))\
              .then_inc(in_w6, 16)
            sp.wait_ge(x_final, 1)
            sp.dma_start(out.rearrange("b (t p) d -> p (b t) d", p=P), x[:, :, :]).then_inc(out_stored, 16)
            sp.wait_ge(out_stored, 16)

        @block.gpsimd
        def _(pool):
            link = Link(pool, pool_link)
            nc.gpsimd.memset(minus_half[:, :], -0.5).then_inc(setup, 1)
            nc.gpsimd.memset(half[:, :], 0.5).then_inc(setup, 1)
            nc.gpsimd.memset(ones[:, :], 1.0).then_inc(setup, 1)
            pool.wait_ge(setup, 3)

            def inverse_root(n):
                pool.wait_ge(ln_var, n + 1)
                nc.gpsimd.tensor_tensor(out=rstd[:, :], in0=var_eps[:, :], in1=minus_half[:, :], op=ALU.pow)\
                  .then_inc(ln_rstd, 1)

            def carry_wait():
                nc.gpsimd.tensor_tensor(out=small[0:1, 3:4], in0=half[0:1, 0:1], in1=half[0:1, 0:1], op=ALU.add)

            inverse_root(0)
            pool.wait_ge(in_mask, 16)
            for t in range(QT):
                nc.gpsimd.tensor_scalar(maskN[:, t, :], mask_raw[:, t, :], 0.0, MASKED, ALU.is_equal, ALU.mult)\
                  .then_inc(mask_ready, 1)
            with pool.Fori(0, B) as b:
                with pool.Fori(0, NCH // B // 2) as j:
                    for s in range(2):
                        pool.wait_ge(low_ready, b * (NCH // B) + 2 * j + s + 1)
                        for part in range(3):
                            pool.dma_start(
                                keys_dram[part, bass.ds(b * D, D), bass.ds((2 * j + s) * CH, CH)]
                                .rearrange("(c p) f -> p c f", p=P),
                                split[s][:, part, :, :]).then_inc(stored[s], 16)
            def slab_rows_of_ones(slots):
                for s in slots:
                    nc.gpsimd.memset(slab[s][KROWS:KALL, :], 1.0).then_inc(slab_ones, 1)
                    pool.wait_ge(slab_ones, s + 1)

            inverse_root(1)
            inverse_root(2)
            pool.wait_ge(xn_ready, 3)
            slab_rows_of_ones(range(2))
            inverse_root(3)
            pool.wait_ge(v_blank, 1)
            pool.wait_ge(in_ctx, 32)
            for u in range(2):
                nc.gpsimd.tensor_copy(vaug[u][:, :, 0:DH4], ctx_nat[:, :, u * DH4:(u + 1) * DH4])\
                  .then_inc(v_ready, 1)
            pool.wait_ge(v_ready, 2)
            slab_rows_of_ones(range(2, RING))
            with pool.Fori(0, U4 // 2 - 1) as i:
                for s in range(2):
                    pool.wait_ge(v_ready, 2 * i + s + 2)
                    pool.wait_ge(pv_psum, 2 * i + s + 1)
                    carry_wait()
                    nc.gpsimd.tensor_copy(vaug[s][:, :, 0:DH4], ctx_nat[:, :, bass.ds((2 * i + s + 2) * DH4, DH4)])\
                      .then_inc(v_ready, 1)
            inverse_root(4)
            pool.wait_ge(pow_arg, 1)
            nc.gpsimd.tensor_tensor(out=root6[:, TT:], in0=square6[:, TT:], in1=half[:, TT:], op=ALU.pow)\
              .then_inc(pow_ready, 1)
            inverse_root(5)
            pool.wait_ge(pow_arg, 2)
            nc.gpsimd.tensor_tensor(out=root6[:, 0:TT], in0=square6[:, 0:TT], in1=half[:, 0:TT], op=ALU.pow)\
              .then_inc(pow_ready, 1)

        @block.scalar
        def _(act):
            def norm_out(n):
                act.wait_ge(xnT_psum, n + 1)
                nc.scalar.activation(xnT[:, :, :], bank[:, 0:2, :], ACT.Copy).then_inc(xnT_ready, 1)

            norm_out(0)
            def ctxT_out(s, c):
                act.wait_ge(ctxT_psum, c + 1)
                act.wait_ge(rest_ready, c)
                nc.scalar.activation(ctxT[s % 2], bank[:, 6 * (s % 2):6 * (s % 2) + 2, :], ACT.Copy)\
                  .then_inc(ctxT_ready, 1)

            def turn1(i, more):
                for s in range(SLOTS1):
                    c = SLOTS1 * i + s
                    for p in range(2):
                        act.wait_ge(h1_ready, 2 * c + p + 1)
                        nc.scalar.activation(geluT[p].rearrange("p a b -> p (a b)"), bank[:, 2 + p, :],
                                             ACT.Gelu_apprx_tanh).then_inc(gelu_ready, 1)
                    if more or s < SLOTS1 - 1:
                        ctxT_out(s + 1, c + 1)
                    act.wait_ge(rest_ready, c + 2)
                    nc.scalar.activation(split[s % 2][:, 1, :, :], rest[s % 2], ACT.Copy).then_inc(mid_ready, 1)
            act.wait_ge(ctxT_psum, 1)
            nc.scalar.activation(ctxT[0], bank[:, 0:2, :], ACT.Copy).then_inc(ctxT_ready, 1)
            with act.Fori(0, TURNS1 - 1) as i:
                turn1(i, True)
            turn1(TURNS1 - 1, False)
            for g in range(GROUPS * 2):
                act.wait_ge(maskT_psum, g + 1)
                nc.scalar.activation(maskT[:, 2 * g:2 * g + 2, :].rearrange("p a b -> p (a b)"),
                                     bf16_bank(2 + g % 2)[:, 0:512], ACT.Copy).then_inc(maskT_ready, 1)
            act.wait_ge(wout_psum, 1)
            nc.scalar.activation(woutT[:, :, :], bank[:, 4:6, 0:D], ACT.Copy).then_inc(wout_ready, 1)

            norm_out(1)
            act.wait_ge(in_w2, 16 * N_W2)
            act.wait_ge(down_psum, 1)
            nc.scalar.activation(downT[0:96, :], bank[0:96, 2, :], ACT.Identity, bias=bdown[:, :])\
              .then_inc(down_ready, 1)

            def heads_out(h):
                s = h % 2
                act.wait_ge(proj2_psum, h + 1)
                nc.scalar.activation(qT2[s], bank[:, 3, :], ACT.Identity, bias=bq2[:, h:h + 1])
                nc.scalar.activation(kT2[s], bank[:, 4, :], ACT.Identity, bias=bk2[:, h:h + 1])
                nc.scalar.activation(qrT2[s][64:96, :], bank[64:96, 5, :], ACT.Identity,
                                     bias=bqr2[64:96, h:h + 1]).then_inc(proj2_ready, 1)

            def exps(n):
                s = n % 2
                act.wait_ge(nmax2, n + 1)
                for t in range(QT):
                    e = nc.scalar.activation(p2[s][:, t, :], bank[:, 6 + s, t * S:(t + 1) * S], ACT.Exp,
                                             bias=sm2[s][:, 1, t:t + 1], scale=SCALE2,
                                             accum_out=sm2[s][:, 2, t:t + 1])
                e.then_inc(exp2, 1)

            def values_out(n):
                act.wait_ge(o2_psum, n + 1)
                nc.scalar.activation(oT2[:, n // B, (n % B) * S:(n % B + 1) * S], bank[:, 2, 0:S], ACT.Copy)\
                  .then_inc(o2_ready, 1)

            heads_out(0)
            exps(0)
            for n in range(UNITS2):
                if n + 1 < UNITS2:
                    if (n + 1) % B == 0:
                        heads_out((n + 1) // B)
                    exps(n + 1)
                if n > 0:
                    values_out(n - 1)
            values_out(UNITS2 - 1)

            norm_out(2)
            act.wait_ge(logit3, 1)
            nc.scalar.activation(prob[:, :, 0:E3], prob[:, :, 0:E3], ACT.Exp).then_inc(exp3, 1)

            def silus(k0):
                for f in range(FT):
                    m = P if f < FT - 1 else FLAST
                    act.wait_ge(gate_psum, k0 + f + 1)
                    nc.scalar.activation(silu[f % 2][0:m, :], bank[0:m, f % 2, :], ACT.Silu).then_inc(silu_ready, 1)
            silus(0)
            with act.Fori(0, E3 // 2) as i:
                for s in range(2):
                    silus(2 * FT * i + FT * (s + 1))

            norm_out(3)
            for n in range(TT * 2):
                t, half_h = n // 2, n % 2
                act.wait_ge(qT_psum, n + 1)
                u0 = (t // QT) * H4 + half_h * 8
                nc.scalar.activation(qT4[0:KROWS, u0:u0 + 8, (t % QT) * P:(t % QT + 1) * P],
                                     bf16_bank(2 + n % 2)[0:KROWS, :].rearrange("p (h q) -> p h q", h=8),
                                     ACT.Copy).then_inc(qT_ready, 1)

            def softmax_numerators(n0):
                for g in range(GROUPS):
                    act.wait_ge(score4, n0 + g + 1)
                    nc.scalar.activation(prob4[g % 2].rearrange("p a b -> p (a b)"),
                                         bank[:, 2 * (g % 2):2 * (g % 2) + 2, :].rearrange("p a b -> p (a b)"),
                                         ACT.Exp, scale=SCALE4).then_inc(exp4_ready, 1)
            with act.Fori(0, U4 // RING) as i:
                for s in range(RING):
                    softmax_numerators(GROUPS * (RING * i + s))
            act.wait_ge(o4T_psum, 1)
            nc.scalar.activation(o4T, bank[:, 4:6, :], ACT.Copy).then_inc(o4T_ready, 1)

            act.wait_ge(in_gate6, 32)
            nc.scalar.activation(col6[:, 0, :], gates6, ACT.Exp, scale=-1.0).then_inc(gate_exp, 1)
            act.wait_ge(fold_psum, 1)
            for n in range(3):
                nc.scalar.activation(fold[:, n, :, :], bank[:, 2 + 2 * n:4 + 2 * n, 0:2 * NF], ACT.Copy)\
                  .then_inc(fold_ready, 1)
            act.wait_ge(fold_psum, 2)
            nc.scalar.activation(brow[0:1, :, :], bank[0:1, 2:5, 0:2 * NF], ACT.Copy).then_inc(fold_ready, 1)
            norm_out(4)
            for n in range(3):
                for t in range(0, TT, 2):
                    k = n * TT + t
                    act.wait_ge(spec_psum, k + 2)
                    o = 4 * ((k // 2) % 2)
                    nc.scalar.activation(spec[:, n, t:t + 2, :], bank[:, o:o + 2, 0:2 * NF], ACT.Copy)\
                      .then_inc(spec_ready, 1)
            for n in range(3):
                act.wait_ge(mag_ready, n + 1)
                nc.scalar.activation(magr[:, n, :, :], magr[:, n, :, :], ACT.Sqrt).then_inc(root_ready, 1)
            act.wait_ge(o5T_psum, 1)
            nc.scalar.activation(o5T, bank[:, 0:2, :], ACT.Copy).then_inc(o5T_ready, 1)
            nc.scalar.activation(o5n[0:1, :], bank[0:1, 2, :], ACT.Copy).then_inc(o5T_ready, 1)

            norm_out(5)
            act.wait_ge(exp6w_arg, 1)
            nc.scalar.activation(prob[:, :, :], prob[:, :, :], ACT.Exp).then_inc(exp6w, 1)
            act.wait_ge(qk6_psum, 1)
            nc.scalar.activation(qT6[0:HD6, :], bank[0:HD6, 0, :], ACT.Copy)
            nc.scalar.activation(kT6[0:HD6, :], bank[0:HD6, 1, :], ACT.Copy).then_inc(qk6_ready, 1)
            for t in range(TT):
                w = S if t % QT else P
                act.wait_ge(nmax6, t + 1)
                nc.scalar.activation(p6[:, t, 0:w], p6[:, t, 0:w], ACT.Exp, bias=row6[:, 2, t:t + 1],
                                     accum_out=row6[:, 3, t:t + 1]).then_inc(exp6, 1)
            for t in range(TT):
                act.wait_ge(mixT_psum, t + 1)
                nc.scalar.activation(mixT[t % 2], bank[:, 2 * (t % 2):2 * (t % 2) + 2, :].rearrange("p a (j q) -> p (a j) q", q=P),
                                     ACT.Copy).then_inc(mixT_ready, 1)

        @block.tensor
        def _(pe):
            mm = nc.tensor.matmul

            def norm_T(n):
                pe.wait_ge(xn_ready, n + 1)
                for t in range(TT):
                    for c in range(DC):
                        last = nc.tensor.transpose(bank[:, c, t * P:(t + 1) * P], xn[:, t, c * P:(c + 1) * P], ident[:, :])
                last.then_inc(xnT_psum, 1)
                pe.wait_ge(xnT_ready, n + 1)

            pe.wait_ge(in_const, 16 * N_CONST)
            pe.wait_ge(setup, 3)
            pe.wait_ge(identb_ready, 1)
            norm_T(0)
            def ctx_T(s, c, fills):
                pe.wait_ge(ctx_loaded[s], 16 * fills)
                for t in range(4):
                    for d in range(DC):
                        last = nc.tensor.transpose(bank[:, 6 * (s % 2) + d, t * P:(t + 1) * P],
                                                   ctx_in[s][:, t, d * P:(d + 1) * P], ident[:, :])
                last.then_inc(ctxT_psum, 1)

            def turn1(b, i, more):
                for s in range(SLOTS1):
                    c = SLOTS1 * i + s
                    pe.wait_ge(ctxT_ready, c + 1)
                    for p in range(2):
                        for t in range(2):
                            f = (2 * p + t) * P
                            for d in range(DC):
                                last = mm(bank[:, 2 + p, t * S:(t + 1) * S], ctxT[s % 2][:, d, f:f + P],
                                          xnT[:, d, b * S:(b + 1) * S], start=(d == 0), stop=(d == DC - 1))
                        last.then_inc(h1_ready, 1)
                    if more or s < SLOTS1 - 1:
                        s1 = (s + 1) % SLOTS1
                        ctx_T(s1, c + 1, i + 1 if s1 else i + 2)
                    if s == 0:
                        pe.wait_ge(x_added1, i + 1)
                    for p in range(2):
                        pe.wait_ge(gelu_ready, 2 * c + p + 1)
                        for t in range(2):
                            for q in range(QT):
                                last = mm(bank[:, 4 + q, 0:D], geluT[p][:, t, q * P:(q + 1) * P],
                                          ctx_in[s][:, 2 * p + t, :], start=(s + p + t == 0),
                                          stop=(s == SLOTS1 - 1 and p + t == 2))
                        last.then_inc(out1_pair, 1)
            ctx_T(0, 0, 1)
            with pe.Fori(0, TPB) as i:
                turn1(0, i, True)
            for i in range(TPB, TURNS1):
                turn1(1, i, i < TURNS1 - 1)
            pe.wait_ge(mask_ready, QT)
            pe.wait_ge(x_added1, TURNS1 + 1)
            for g in range(GROUPS * 2):
                if g >= 2:
                    pe.wait_ge(maskT_ready, g - 1)
                for k in range(2):
                    for q in range(QT):
                        f = (2 * g + k) * P
                        last = nc.tensor.transpose(bf16_bank(2 + g % 2)[:, k * S + q * P:k * S + (q + 1) * P],
                                                   maskN[:, q, f:f + P], identb[:, :])
                last.then_inc(maskT_psum, 1)
            pe.wait_ge(in_wout, 16)
            for c in range(DC):
                for o in range(DC):
                    last = nc.tensor.transpose(bank[:, 4 + c, o * P:(o + 1) * P], wout[:, o, c * P:(c + 1) * P], ident[:, :])
            last.then_inc(wout_psum, 1)

            pe.wait_ge(maskT_ready, GROUPS * 2)
            pe.wait_ge(wout_ready, 1)
            norm_T(1)
            pe.wait_ge(in_w2, 16 * N_W2)
            for c in range(DC):
                last = mm(bank[0:96, 2, :], wdown[:, c, :], xnT[:, c, :], start=(c == 0), stop=(c == DC - 1))
            last.then_inc(down_psum, 1)
            pe.wait_ge(down_ready, 1)

            def heads(h):
                if h > 0:
                    pe.wait_ge(proj2_ready, h)
                w = slice(h * DK, (h + 1) * DK)
                mm(bank[:, 3, :], up[0:32, 0, w], downT[0:32, :], start=True, stop=True)
                mm(bank[:, 4, :], up[32:64, 0, w], downT[32:64, :], start=True, stop=True)
                mm(bank[64:96, 5, :], up[0:32, 1, h * DR:(h + 1) * DR], downT[0:32, :], start=True, stop=True)\
                    .then_inc(proj2_psum, 1)

            def scores(n):
                h, b = n // B, n % B
                if b == 0:
                    pe.wait_ge(proj2_ready, h + 1)
                for q in range(QT):
                    o = bank[:, 6 + n % 2, q * S:(q + 1) * S]
                    t = b * S + q * P
                    mm(o, qT2[h % 2][:, t:t + P], kT2[h % 2][:, b * S:(b + 1) * S], start=True, stop=False)
                    last = mm(o, qrT2[h % 2][64:96, t:t + P], downT[64:96, b * S:(b + 1) * S], start=False, stop=True)
                last.then_inc(score2, 1)

            def values2(n):
                h, b = n // B, n % B
                pe.wait_ge(pT2_ready, n + 1)
                if n > 0:
                    pe.wait_ge(o2_ready, n)
                for k in range(2):
                    last = mm(bank[:, 2, 0:S], v2[:, b * QT + k, h * DK:(h + 1) * DK], pT2[n % 2][:, k, :],
                              start=(k == 0), stop=(k == 1))
                last.then_inc(o2_psum, 1)

            for n in range(TT * 2):
                if n >= 2:
                    pe.wait_ge(v2_ready, n - 1)
                t, c = n // 2, n % 2
                mm(bank[:, n % 2, :], downT[32:64, t * P:(t + 1) * P], up[32:64, 1, c * 512:(c + 1) * 512],
                   start=True, stop=True).then_inc(v2_psum, 1)
            heads(0)
            scores(0)
            pe.wait_ge(v2_ready, TT * 2)
            for n in range(UNITS2):
                h, b = n // B, n % B
                if n + 1 < UNITS2:
                    if (n + 1) % B == 0:
                        heads((n + 1) // B)
                    scores(n + 1)
                pe.wait_ge(norm2, n + 1)
                for k in range(2):
                    for q in range(QT):
                        last = nc.tensor.transpose(bank[:, n % 2, k * S + q * P:k * S + (q + 1) * P],
                                                   p2[n % 2][:, q, k * P:(k + 1) * P], ident[:, :])
                last.then_inc(pT2_psum, 1)
                if n > 0:
                    values2(n - 1)
            values2(UNITS2 - 1)
            pe.wait_ge(o2_ready, UNITS2)
            pe.wait_ge(in_wo2, 16)
            for t in range(TT):
                for h in range(H2):
                    last = mm(bank[:, 3 + t, 0:D], oT2[:, h, t * P:(t + 1) * P], wo2[:, h, :],
                              start=(h == 0), stop=(h == H2 - 1))
                last.then_inc(y2_psum, 1)

            norm_T(2)
            pe.wait_ge(in_gate3, 16 * DC)
            for t in range(TT):
                for c in range(DC):
                    last = mm(bank[:, 7, t * 16:t * 16 + E3], xnT[:, c, t * P:(t + 1) * P], gate3[:, c, :],
                              start=(c == 0), stop=(c == DC - 1))
            last.then_inc(logit3_psum, 1)

            def down3(s, n, f, k0):
                m = P if f < FT - 1 else FLAST
                pe.wait_ge(hid_ready, k0 + f + 1)
                if f == 0:
                    pe.wait_ge(y3_added, n)
                for t in range(TT):
                    last = mm(bank[:, 4 + t, 0:D], hid[f % 2][0:m, t * P:(t + 1) * P], w3[s][2][0:m, f, :],
                              start=(f == 0), stop=(f == FT - 1))
                if f == FT - 1:
                    last.then_inc(y3_psum, 1)

            def expert(s, n, fills):
                k0 = n * FT
                pe.wait_ge(in_w3[s], fills * 64)
                for f in range(FT):
                    m = P if f < FT - 1 else FLAST
                    for w, o, done in ((0, 0, gate_psum), (1, 2, up_psum)):
                        for c in range(DC):
                            last = mm(bank[0:m, o + f % 2, :], w3[s][w][:, c, f * P:f * P + m], xnT[:, c, :],
                                      start=(c == 0), stop=(c == DC - 1))
                        last.then_inc(done, 1)
                    if f > 0:
                        down3(s, n, f - 1, k0)
                down3(s, n, FT - 1, k0)
            expert(0, 0, 1)
            with pe.Fori(0, E3 // 2) as i:
                expert(1, 2 * i + 1, i + 1)
                expert(0, 2 * i + 2, i + 2)

            norm_T(3)
            pe.wait_ge(q_rows_ready, 1)
            for n in range(TT * 2):
                if n >= 2:
                    pe.wait_ge(qT_ready, n - 1)
                t, hh = n // 2, n % 2
                for h in range(8):
                    last = nc.tensor.transpose(bf16_bank(2 + n % 2)[0:KROWS, h * P:(h + 1) * P],
                                               q_rows[:, t, hh * 8 + h, :], identb[:, :])
                last.then_inc(qT_psum, 1)
            pe.wait_ge(qT_ready, TT * 2)
            pe.wait_ge(slab_ones, 2)

            def max_piece(s, u, m):
                q, c = m % 2, m // 2
                k = u * MAXES + m
                if not isinstance(k, int) or k >= 2:
                    pe.wait_ge(max_taken, k - 1)
                mm(bank[:, 4 + q, :], qT4[0:KROWS, bass.ds(u, 1), q * P:(q + 1) * P].rearrange("p o q -> p (o q)"),
                   slab[s][0:KROWS, c * CH:(c + 1) * CH], start=True, stop=True).then_inc(max_psum, 1)

            def negmax_T(u):
                pe.wait_ge(negmax_ready, u + 1)
                for q in range(QT):
                    last = nc.tensor.transpose(bf16_bank(7)[KROWS:KALL, q * P:(q + 1) * P], negparts[:, q, 0:3],
                                               identb[:, :])
                last.then_inc(negT_psum, 1)

            def score_products(s, u, g):
                for k in range(4):
                    mm(bank[:, 2 * (g % 2) + k // 2, (k % 2) * S:(k % 2 + 1) * S],
                       slab[s][0:KALL, (4 * g + k) * P:(4 * g + k + 1) * P],
                       qT4[0:KALL, bass.ds(u, 1), :].rearrange("p o q -> p (o q)"),
                       start=(k % 2 == 0), stop=False, skip_group_check=True)

            def score_mask(g):
                for k in range(2):
                    last = mm(bank[:, 2 * (g % 2) + k, :], identb[:, :],
                              maskT[:, 4 * g + 2 * k:4 * g + 2 * k + 2, :].rearrange("p a b -> p (a b)"),
                              start=False, stop=True, skip_group_check=True)
                last.then_inc(score4, 1)

            def values_group(s, n0, g):
                pe.wait_ge(exp4_ready, n0 + g + 1)
                for k in range(4):
                    last = mm(bank[32 * k:32 * k + 32, 6, 0:S], vaug[s][:, 4 * g + k, :], prob4[g % 2][:, k, :],
                              start=(g == 0), stop=(g == GROUPS - 1), skip_group_check=True)
                if g == GROUPS - 1:
                    last.then_inc(pv_psum, 1)

            def unit(s, u, fills, left=3):
                s1, s2 = (s + 1) % RING, (s + 2) % RING

                def slab_there(r):
                    pe.wait_ge(slab_loaded[r], (fills + (1 if r < s else 0)) * 16 * TERMS)

                def piece(g, n):
                    m = AHEAD + 2 * g + n
                    if m < MAXES:
                        if left >= 1:
                            max_piece(s1, u + 1, m)
                    elif left >= 2:
                        max_piece(s2, u + 2, m - MAXES)
                for g in range(GROUPS):
                    if left >= 2 and 2 * g + AHEAD == MAXES:
                        slab_there(s2)
                    if g < GROUPS - 1:
                        piece(g, 0)
                        score_products(s, u, g + 1)
                        piece(g, 1)
                        score_mask(g + 1)
                    if g == 0:
                        pe.wait_ge(v_ready, u + 1)
                        pe.wait_ge(pv_copied, u + 1)
                    if g == GROUPS - 1:
                        piece(g, 0)
                    values_group(s % 2, GROUPS * u, g)
                    if left >= 1 and g == GROUPS - 2:
                        negmax_T(u + 1)
                if left >= 1:
                    pe.wait_ge(negT_ready, u + 2)
                    score_products(s1, u + 1, 0)
                piece(GROUPS - 1, 1)
                if left >= 1:
                    score_mask(0)
                pe.wait_ge(pv_copied, u + 2)
                for q in range(QT):
                    last = nc.tensor.transpose(bank[:, 7, 256 + q * P:256 + (q + 1) * P], pv_sb[:, q * P:(q + 1) * P],
                                               ident[:, :])
                last.then_inc(oT_psum, 1)

            pe.wait_ge(slab_loaded[0], 16 * TERMS)
            for m in range(MAXES):
                max_piece(0, 0, m)
            pe.wait_ge(slab_loaded[1], 16 * TERMS)
            for m in range(AHEAD):
                max_piece(1, 1, m)
            negmax_T(0)
            pe.wait_ge(negT_ready, 1)
            score_products(0, 0, 0)
            score_mask(0)
            pe.wait_ge(slab_ones, RING)
            with pe.Fori(0, U4 // RING - 1) as i:
                for s in range(RING):
                    unit(s, RING * i + s, i + 1)
            for s in range(RING):
                unit(s, U4 - RING + s, U4 // RING, RING - 1 - s)
            pe.wait_ge(o4_ready, 1)
            for t in range(TT):
                for c in range(DC):
                    o = (t // QT) * D + c * P
                    last = nc.tensor.transpose(bank[:, 4 + c, t * P:(t + 1) * P], o4[:, t % QT, o:o + P], ident[:, :])
            last.then_inc(o4T_psum, 1)
            pe.wait_ge(o4T_ready, 1)
            for t in range(TT):
                for c in range(DC):
                    last = mm(bank[:, t // 2, (t % 2) * D:(t % 2 + 1) * D], o4T[:, c, t * P:(t + 1) * P], woutT[:, c, :],
                              start=(c == 0), stop=(c == DC - 1))
                last.then_inc(y4_psum, 1)

            pe.wait_ge(in_w5, 16 * N_W5)
            for n in range(3):
                for o in range(DC):
                    for c in range(DC):
                        last = mm(bank[:, 2 + 2 * n + o, 0:2 * NF], w5[:, n, c, o * P:(o + 1) * P], dft[:, c, :],
                                  start=(c == 0), stop=(c == DC - 1))
            last.then_inc(fold_psum, 1)
            pe.wait_ge(fold_ready, 3)
            for n in range(3):
                for c in range(DC):
                    last = mm(bank[0:1, 2 + n, 0:2 * NF], b5[:, n, c:c + 1], dft[:, c, :],
                              start=(c == 0), stop=(c == DC - 1))
            last.then_inc(fold_psum, 1)
            pe.wait_ge(fold_ready, 4)
            norm_T(4)
            pe.wait_ge(sim_sq, 1)
            for c in range(DC):
                last = mm(bank[:, 3, 0:E6], ones[:, :], sim2[:, c, :], start=(c == 0), stop=(c == DC - 1))
            last.then_inc(norm6_psum, 1)
            for n in range(3):
                for t in range(TT):
                    k = n * TT + t
                    o = bank[:, 4 * ((k // 2) % 2) + k % 2, 0:2 * NF]
                    if k >= 4 and k % 2 == 0:
                        pe.wait_ge(spec_ready, k // 2 - 1)
                    for c in range(DC):
                        mm(o, xnT[:, c, t * P:(t + 1) * P], fold[:, n, c, :], start=(c == 0), stop=False)
                    mm(o, ones[0:1, :], brow[0:1, n, :], start=False, stop=True).then_inc(spec_psum, 1)
            pe.wait_ge(spec_ready, 6)
            pe.wait_ge(z_ready, 1)
            for t in range(TT):
                o = bank[:, 4 + t, 0:2 * NF]
                if t % QT:
                    mm(o, ones[:, :], z5[:, t - 1, :], start=True, stop=False)
                mm(o, tri[:, :], z5[:, t, :], start=(t % QT == 0), stop=True).then_inc(sum_psum, 1)
            pe.wait_ge(o5_ready, 1)
            for t in range(TT):
                nc.tensor.transpose(bank[:, 0, t * P:(t + 1) * P], t5[:, t, 0:P], ident[:, :])
                nc.tensor.transpose(bank[:, 1, t * P:(t + 1) * P], t5[:, t, NF:NF + P], ident[:, :])
                last = nc.tensor.transpose(bank[0:1, 2, t * P:(t + 1) * P], t5[:, t, NF - 1:NF], ident[:, :])
            last.then_inc(o5T_psum, 1)
            pe.wait_ge(o5T_ready, 2)
            for t in range(TT):
                for c in range(DC):
                    mm(bank[:, 4 + t, 0:D], o5T[:, c, t * P:(t + 1) * P], idft[:, c, :], start=(c == 0), stop=False)
                mm(bank[:, 4 + t, 0:D], o5n[0:1, t * P:(t + 1) * P], idft_ny[0:1, :], start=False, stop=True)\
                    .then_inc(y5_psum, 1)

            norm_T(5)
            pe.wait_ge(in_w6, 16 * N_W6)
            for t in range(TT):
                for c in range(DC):
                    last = mm(bank[:, 2, t * E6:(t + 1) * E6], xnT[:, c, t * P:(t + 1) * P], sim6[:, c, :],
                              start=(c == 0), stop=(c == DC - 1))
            last.then_inc(logit6_psum, 1)
            for k in range(TT * E6 // 2):
                t, e = k // (E6 // 2), 2 * (k % (E6 // 2))
                if k >= len(DEEP6):
                    pe.wait_ge(proj6_used, k - len(DEEP6) + 1)
                for c in range(DC):
                    last = mm(bank[:, DEEP6[k % len(DEEP6)], 0:2 * QKV], xnT[:, c, t * P:(t + 1) * P],
                              w6[:, c, e:e + 2, :].rearrange("p a b -> p (a b)"), start=(c == 0), stop=(c == DC - 1))
                last.then_inc(proj6, 1)
            pe.wait_ge(qkv_ready, 1)
            for t in range(TT):
                nc.tensor.transpose(bank[0:HD6, 0, t * P:(t + 1) * P], qkv[:, t, 0:HD6], ident[:, :])
                last = nc.tensor.transpose(bank[0:HD6, 1, t * P:(t + 1) * P], qkv[:, t, HD6:2 * HD6], ident[:, :])
            last.then_inc(qk6_psum, 1)
            pe.wait_ge(qk6_ready, 1)
            for t in range(TT):
                w = S if t % QT else P
                b = t // QT
                mm(bank[:, 4 + t, 0:w], qT6[0:HD6, t * P:(t + 1) * P], kT6[0:HD6, b * S:b * S + w],
                   start=True, stop=True).then_inc(score6, 1)
            for t in range(TT):
                pe.wait_ge(norm6, t + 1)
                for k in range(t % QT + 1):
                    last = nc.tensor.transpose(bank[:, t % 2, k * P:(k + 1) * P], p6[:, t, k * P:(k + 1) * P], ident[:, :])
                last.then_inc(pT6_psum, 1)
                pe.wait_ge(pT6_ready, t + 1)
                for k in range(t % QT + 1):
                    last = mm(bank[:, 4 + t, 0:HD6], pT6[:, t, k, :], qkv[:, (t // QT) * QT + k, 2 * HD6:QKV],
                              start=(k == 0), stop=(k == t % QT))
                last.then_inc(att6, 1)
            def mix_T(t):
                pe.wait_ge(mix_ready, t + 1)
                for j in range(8):
                    last = nc.tensor.transpose(bank[:, 2 * (t % 2) + j // 4, (j % 4) * P:(j % 4 + 1) * P],
                                               mixed[t % 2][:, j * P:(j + 1) * P], ident[:, :])
                last.then_inc(mixT_psum, 1)
            mix_T(0)
            for t in range(TT):
                if t + 1 < TT:
                    mix_T(t + 1)
                pe.wait_ge(mixT_ready, t + 1)
                for j in range(8):
                    last = mm(bank[:, 4 + t, 0:D], mixT[t % 2][:, j, :], wo6[:, j, :], start=(j == 0), stop=(j == 7))
                last.then_inc(y6_psum, 1)

        @block.vector
        def _(dve):
            v = nc.vector
            link = Link(dve, dve_link)

            def layer_norm(n):
                for t in range(TT):
                    last = v.bn_stats(stats[:, t, :], x[:, t, :])
                link(last)
                for t in range(TT):
                    last = v.bn_aggr(moments[:, t, :], stats[:, t, :])
                link(last)
                v.tensor_scalar(var_eps[:, :], moments[:, :, 1], EPS, None, ALU.add).then_inc(ln_var, 1)
                dve.wait_ge(ln_rstd, n + 1)
                for t in range(TT):
                    last = v.tensor_scalar(xn[:, t, :], x[:, t, :], moments[:, t, 0:1], rstd[:, t:t + 1],
                                           ALU.subtract, ALU.mult)
                last.then_inc(xn_ready, 1)
                dve.wait_ge(xn_ready, n + 1)

            def wide(r, n):
                return r.unsqueeze(2).broadcast_to([P, TT, n])

            def top2(vals, n, low):
                eq, rank, first, second = (pick[:, k, :, 0:n] for k in range(4))
                order = rev[:, 0:n].unsqueeze(1).broadcast_to([P, TT, n])
                for k, hot in enumerate((first, second)):
                    src = vals if k == 0 else eq
                    link(v.tensor_reduce(red[:, 0, :], src, AX.X, ALU.max))
                    link(v.tensor_tensor(rank, src, wide(red[:, 0, :], n), ALU.is_equal))
                    link(v.tensor_tensor(rank, rank, order, ALU.mult))
                    link(v.tensor_reduce(red[:, 1, :], rank, AX.X, ALU.max))
                    link(v.tensor_tensor(hot, rank, wide(red[:, 1, :], n), ALU.is_equal))
                    if k == 0:
                        link(v.tensor_scalar(eq, hot, low, None, ALU.mult))
                        link(v.tensor_tensor(eq, eq, vals, ALU.add))
                link(v.tensor_tensor(first, first, second, ALU.add))
                return first

            dve.wait_ge(in_const, 16 * N_CONST)
            v.tensor_copy(identb[:, :], ident[:, :]).then_inc(identb_ready, 1)
            v.memset(small[0:1, 0:1], 0.0).then_inc(x_added1, 1)
            v.memset(small[0:1, 1:2], 0.0).then_inc(pv_copied, 1)
            v.memset(small[0:1, 2:3], 0.0).then_inc(rest_ready, 1)
            dve.wait_ge(in_x, 16)
            layer_norm(0)

            def turn1(b, i, first=False):
                for s in range(SLOTS1):
                    c, r = SLOTS1 * i + s, s % 2
                    dve.wait_ge(ctxT_ready, c + 1)
                    if not first or s >= 2:
                        dve.wait_ge(stored[r], 48 * (SLOTS1 // 2 * i + s // 2))
                    v.tensor_copy(split[r][:, 0, :, :], ctxT[r]).then_inc(high_ready, 1)
                    dve.wait_ge(high_ready, c + 1)
                    v.tensor_tensor(rest[r], ctxT[r], split[r][:, 0, :, :], ALU.subtract).then_inc(rest_ready, 1)
                    dve.wait_ge(mid_ready, c + 1)
                    v.tensor_tensor(split[r][:, 2, :, :], rest[r], split[r][:, 1, :, :], ALU.subtract)\
                     .then_inc(low_ready, 1)
                dve.wait_ge(out1_pair, 2 * SLOTS1 * (i + 1))
                dve.wait_ge(x_added1, i + 1)
                xs = x[:, b * QT:(b + 1) * QT, :]
                v.tensor_tensor(xs, xs, bank[:, 4:6, 0:D], ALU.add).then_inc(x_added1, 1)
            turn1(0, 0, True)
            with dve.Fori(1, TPB) as i:
                turn1(0, i)
            with dve.Fori(TPB, TURNS1) as i:
                turn1(1, i)
            dve.wait_ge(x_added1, TURNS1 + 1)

            layer_norm(1)
            dve.wait_ge(in_w2, 16 * N_W2)
            link(v.tensor_tensor(x[:, :, :], x[:, :, :], bo2.unsqueeze(1).broadcast_to([P, TT, D]), ALU.add))
            for n in range(TT * 2):
                t, c = n // 2, n % 2
                dve.wait_ge(v2_psum, n + 1)
                v.tensor_tensor(v2[:, t, c * 512:(c + 1) * 512], bank[:, n % 2, :], bv2[:, c * 512:(c + 1) * 512],
                                ALU.add).then_inc(v2_ready, 1)

            def max2(n):
                s = n % 2
                dve.wait_ge(score2, n + 1)
                link(v.tensor_reduce(sm2[s][:, 0, :], bank[:, 6 + s, :].rearrange("p (q k) -> p q k", q=QT), AX.X, ALU.max))
                v.tensor_scalar(sm2[s][:, 1, :], sm2[s][:, 0, :], -SCALE2, None, ALU.mult).then_inc(nmax2, 1)
            max2(0)
            for n in range(UNITS2):
                s = n % 2
                dve.wait_ge(exp2, n + 1)
                link(v.reciprocal(sm2[s][:, 3, :], sm2[s][:, 2, :]))
                v.tensor_tensor(p2[s], p2[s], sm2[s][:, 3, :].unsqueeze(2).broadcast_to([P, QT, S]), ALU.mult)\
                 .then_inc(norm2, 1)
                if n + 1 < UNITS2:
                    max2(n + 1)
                dve.wait_ge(pT2_psum, n + 1)
                v.tensor_copy(pT2[s].rearrange("p a b -> p (a b)"), bank[:, s, :]).then_inc(pT2_ready, 1)
            for t in range(TT):
                dve.wait_ge(y2_psum, t + 1)
                link(v.tensor_tensor(x[:, t, :], x[:, t, :], bank[:, 3 + t, 0:D], ALU.add))

            layer_norm(2)
            dve.wait_ge(logit3_psum, 1)
            logits = bank[:, 7, 0:TT * 16].rearrange("p (t e) -> p t e", t=TT)[:, :, 0:E3]
            link(v.tensor_reduce(red[:, 0, :], logits, AX.X, ALU.max))
            v.tensor_tensor(prob[:, :, 0:E3], logits, wide(red[:, 0, :], E3), ALU.subtract).then_inc(logit3, 1)

            def hiddens(k0):
                for f in range(FT):
                    m = P if f < FT - 1 else FLAST
                    dve.wait_ge(up_psum, k0 + f + 1)
                    dve.wait_ge(silu_ready, k0 + f + 1)
                    v.tensor_tensor(hid[f % 2][0:m, :], silu[f % 2][0:m, :], bank[0:m, 2 + f % 2, :], ALU.mult)\
                     .then_inc(hid_ready, 1)
            hiddens(0)
            dve.wait_ge(y3_psum, 1)
            v.tensor_tensor(x[:, :, :], x[:, :, :], bank[:, 4:8, 0:D], ALU.add).then_inc(y3_added, 1)
            dve.wait_ge(exp3, 1)
            pr = prob[:, :, 0:E3]
            link(v.tensor_reduce(red[:, 0, :], pr, AX.X, ALU.add))
            link(v.reciprocal(red[:, 1, :], red[:, 0, :]))
            link(v.tensor_tensor(pr, pr, wide(red[:, 1, :], E3), ALU.mult))
            chosen = top2(pr, E3, -4.0)
            w = weight[:, :, 0:E3]
            link(v.tensor_tensor(w, chosen, pr, ALU.mult))
            link(v.tensor_reduce(red[:, 0, :], w, AX.X, ALU.add))
            link(v.tensor_scalar(red[:, 0, :], red[:, 0, :], 1e-20, None, ALU.add))
            link(v.reciprocal(red[:, 1, :], red[:, 0, :]))
            link(v.tensor_tensor(w, w, wide(red[:, 1, :], E3), ALU.mult))
            with dve.Fori(0, E3 // 2) as i:
                for s in range(2):
                    n = 2 * i + s + 1
                    hiddens(n * FT)
                    dve.wait_ge(y3_psum, n + 1)
                    dve.wait_ge(y3_added, n)
                    for t in range(TT):
                        last = v.scalar_tensor_tensor(x[:, t, :], bank[:, 4 + t, 0:D],
                                                      weight[:, t, bass.ds(n - 1, 1)], x[:, t, :], ALU.mult, ALU.add)
                    last.then_inc(y3_added, 1)
            dve.wait_ge(y3_added, E3 + 1)

            layer_norm(3)
            xq = xn[:, :, :].rearrange("p t (h d) -> p t h d", d=DH4)
            rest_q = q_rest.rearrange("p t (h d) -> p t h d", d=DH4)

            def term(n):
                return q_rows[:, :, :, n * DH4:(n + 1) * DH4]
            link(v.tensor_copy(term(0), xq))
            link(v.tensor_tensor(rest_q, xq, term(0), ALU.subtract))
            link(v.tensor_copy(term(1), rest_q))
            link(v.tensor_tensor(term(2), rest_q, term(1), ALU.subtract))
            v.tensor_copy(term(3), term(0))
            v.tensor_copy(term(4), term(1))
            v.tensor_copy(term(5), term(0)).then_inc(q_rows_ready, 1)
            for s in range(2):
                v.memset(vaug[s][:, :, DH4 + 1:32], 0.0)
                last = v.memset(vaug[s][:, :, DH4:DH4 + 1], 1.0)
            last.then_inc(v_blank, 1)
            dve.wait_ge(qT_ready, TT * 2)

            def take_max(s, u, m):
                k = u * MAXES + m
                q, c = m % 2, m // 2
                dve.wait_ge(max_psum, k + 1)
                v.memset(small[0:1, 1 + q:2 + q], 0.0)
                v.tensor_tensor_reduce(out=junk[q], in0=bank[:, 4 + q, :], in1=maskN[:, q, c * CH:(c + 1) * CH], scale=1.0,
                                       scalar=-3.0e38, op0=ALU.add, op1=ALU.max, accum_out=cmax[s][:, q, c:c + 1])\
                 .then_inc(max_taken, 1)

            def negmax_parts(s, u):
                dve.wait_ge(max_taken, u * MAXES + MAXES)
                link(v.tensor_reduce(negmax[:, 0, :], cmax[s], AX.X, ALU.max, negate=True))
                link(v.tensor_copy(negparts[:, :, 0], negmax[:, 0, :]))
                link(v.tensor_tensor(negmax[:, 1, :], negmax[:, 0, :], negparts[:, :, 0], ALU.subtract))
                link(v.tensor_copy(negparts[:, :, 1], negmax[:, 1, :]))
                v.tensor_tensor(negparts[:, :, 2], negmax[:, 1, :], negparts[:, :, 1], ALU.subtract)\
                 .then_inc(negmax_ready, 1)

            def negmax_row(u):
                dve.wait_ge(negT_psum, u + 1)
                v.tensor_copy(qT4[KROWS:KALL, bass.ds(u, 1), :].rearrange("p o q -> p (o q)"),
                              bf16_bank(7)[KROWS:KALL, 0:S]).then_inc(negT_ready, 1)

            def unit(s, u, left=2):
                if left >= 1:
                    for m in range(AHEAD, MAXES):
                        take_max(1 - s, u + 1, m)
                    negmax_parts(1 - s, u + 1)
                if left >= 2:
                    for m in range(AHEAD // 2):
                        take_max(s, u + 2, m)
                if left >= 1:
                    negmax_row(u + 1)
                if left >= 2:
                    take_max(s, u + 2, AHEAD // 2)
                dve.wait_ge(pv_psum, u + 1)
                v.tensor_copy(pv_sb, bank[:, 6, 0:S]).then_inc(pv_copied, 1)
                if left >= 2:
                    take_max(s, u + 2, AHEAD // 2 + 1)
                dve.wait_ge(oT_psum, u + 1)
                parts = bank[:, 7, 256:512].rearrange("p (q j d) -> p q d j", q=QT, j=4)[:, :, 0:DH4 + 1, :]
                link(v.tensor_reduce(osum, parts, AX.X, ALU.add))
                link(v.reciprocal(orec, osum[:, :, DH4]))
                v.tensor_tensor(o4[:, :, bass.ds(u * DH4, DH4)], osum[:, :, 0:DH4],
                                orec.unsqueeze(2).broadcast_to([P, QT, DH4]), ALU.mult).then_inc(o4_unit, 1)

            for m in range(MAXES):
                take_max(0, 0, m)
            negmax_parts(0, 0)
            for m in range(AHEAD):
                take_max(1, 1, m)
            negmax_row(0)
            with dve.Fori(0, U4 // 2 - 1) as i:
                link.loop(i, 12)
                for s in range(2):
                    unit(s, 2 * i + s)
            link.end(U4 // 2 - 1)
            unit(0, U4 - 2, 1)
            unit(1, U4 - 1, 0)
            dve.wait_ge(o4_unit, U4)
            dve.wait_ge(in_wout, 32)
            v.tensor_tensor(x[:, :, :], x[:, :, :], bo4.unsqueeze(1).broadcast_to([P, TT, D]), ALU.add)\
             .then_inc(o4_ready, 1)
            dve.wait_ge(o4_ready, 1)
            dve.wait_ge(y4_psum, TT)
            link(v.tensor_tensor(x[:, :, :], x[:, :, :], bank[:, 0:2, :].rearrange("p a (b d) -> p (a b) d", d=D), ALU.add))

            layer_norm(4)
            dve.wait_ge(in_gate6, 32)
            v.tensor_tensor(sim2, sim6, sim6, ALU.mult).then_inc(sim_sq, 1)
            dve.wait_ge(gate_exp, 1)
            link(v.tensor_scalar(col6[:, 2, :], col6[:, 0, :], 1.0, None, ALU.add))
            link(v.reciprocal(col6[:, 3, :], col6[:, 2, :]))
            dve.wait_ge(norm6_psum, 1)
            v.tensor_copy(square6[:, TT:TT + E6], bank[:, 3, 0:E6]).then_inc(pow_arg, 1)
            dve.wait_ge(pow_ready, 1)
            link(v.tensor_scalar(root6[:, TT:], root6[:, TT:], 1e-12, None, ALU.max))
            link(v.reciprocal(root6[:, TT:], root6[:, TT:]))
            for n in range(3):
                dve.wait_ge(mag_ready, n)
                dve.wait_ge(spec_ready, 2 * n + 2)
                link(v.tensor_tensor(mag, spec[:, n, :, :], spec[:, n, :, :], ALU.mult))
                v.tensor_tensor(magr[:, n, :, :], mag[:, :, 0:NF], mag[:, :, NF:2 * NF], ALU.add).then_inc(mag_ready, 1)
            re, im = slice(0, NF), slice(NF, 2 * NF)

            def product(o, l, r, tmp, sign):
                add, sub = (ALU.add, ALU.subtract) if sign > 0 else (ALU.subtract, ALU.add)
                v.tensor_tensor(o[:, :, re], l[:, :, re], r[:, :, re], ALU.mult)
                link(v.tensor_tensor(tmp[:, :, re], l[:, :, im], r[:, :, im], ALU.mult))
                link(v.tensor_tensor(o[:, :, re], o[:, :, re], tmp[:, :, re], sub))
                v.tensor_tensor(o[:, :, im], l[:, :, im], r[:, :, re], ALU.mult)
                link(v.tensor_tensor(tmp[:, :, im], l[:, :, re], r[:, :, im], ALU.mult))
                return v.tensor_tensor(o[:, :, im], o[:, :, im], tmp[:, :, im], add)
            dve.wait_ge(mag_ready, 3)
            link(product(z5, spec[:, 0, :, :], spec[:, 1, :, :], mag, 1))

            def scale_by_inverse(o, m):
                link(v.reciprocal(m, m))
                for c in (re, im):
                    last = v.tensor_tensor(o[:, :, c], o[:, :, c], m, ALU.mult)
                return last
            mk, mv, mq = (magr[:, n, :, :] for n in range(3))
            dve.wait_ge(root_ready, 3)
            link(v.tensor_scalar(mk, mk, 1e-8, None, ALU.add))
            link(v.tensor_scalar(mv, mv, 1e-8, None, ALU.add))
            link(v.tensor_tensor(mv, mv, mk, ALU.mult))
            scale_by_inverse(z5, mv).then_inc(z_ready, 1)
            link(v.tensor_scalar(mq, mq, 1e-8, None, ALU.add))
            link(scale_by_inverse(spec[:, 2, :, :], mq))
            dve.wait_ge(sum_psum, TT)
            product(t5, bank[:, 4:8, 0:2 * NF], spec[:, 2, :, :], mag, -1).then_inc(o5_ready, 1)
            dve.wait_ge(y5_psum, TT)
            link(v.tensor_tensor(x[:, :, :], x[:, :, :], bank[:, 4:8, 0:D], ALU.add))

            layer_norm(5)
            link(v.tensor_tensor(sq6, xn[:, :, :], xn[:, :, :], ALU.mult))
            v.tensor_reduce(square6[:, 0:TT], sq6, AX.X, ALU.add).then_inc(pow_arg, 1)
            dve.wait_ge(pow_ready, 2)
            link(v.tensor_scalar(root6[:, 0:TT], root6[:, 0:TT], 1e-12, None, ALU.max))
            link(v.reciprocal(root6[:, 0:TT], root6[:, 0:TT]))
            dve.wait_ge(logit6_psum, 1)
            lg = bank[:, 2, 0:TT * E6].rearrange("p (t e) -> p t e", t=TT)

            def row(r):
                return r.unsqueeze(1).broadcast_to([P, TT, E6])
            link(v.tensor_tensor(logit6, lg, wide(root6[:, 0:TT], E6), ALU.mult))
            link(v.tensor_tensor(logit6, logit6, row(root6[:, TT:TT + E6]), ALU.mult))
            link(v.tensor_tensor(logit6, logit6, row(col6[:, 3, :]), ALU.subtract))
            fallback = top2(logit6, E6, -1.0e30)
            active, gated, used = (pick[:, k, :, :] for k in (1, 2, 4))
            link(v.tensor_scalar(active, logit6, 0.0, None, ALU.is_gt))
            link(v.tensor_reduce(red[:, 2, :], active, AX.X, ALU.max))
            link(v.tensor_scalar(red[:, 3, :], red[:, 2, :], 0.0, None, ALU.is_equal))
            link(v.tensor_tensor(used, fallback, wide(red[:, 3, :], E6), ALU.mult))
            link(v.tensor_tensor(used, used, active, ALU.add))
            link(v.tensor_scalar(gated, logit6, 0.0, None, ALU.max))
            link(v.tensor_reduce(red[:, 2, :], gated, AX.X, ALU.max))
            v.tensor_tensor(prob[:, :, :], gated, wide(red[:, 2, :], E6), ALU.subtract).then_inc(exp6w_arg, 1)
            dve.wait_ge(exp6w, 1)
            link(v.tensor_tensor(weight[:, :, :], prob[:, :, :], used, ALU.mult))
            link(v.tensor_reduce(red[:, 2, :], weight[:, :, :], AX.X, ALU.add))
            link(v.reciprocal(red[:, 3, :], red[:, 2, :]))
            link(v.tensor_tensor(weight[:, :, :], weight[:, :, :], wide(red[:, 3, :], E6), ALU.mult))
            for k in range(TT * E6 // 2):
                t, e = k // (E6 // 2), 2 * (k % (E6 // 2))
                dve.wait_ge(proj6, k + 1)
                for j in range(2):
                    src = bank[:, DEEP6[k % len(DEEP6)], j * QKV:(j + 1) * QKV]
                    wt = weight[:, t, e + j:e + j + 1]
                    if e + j == 0:
                        link(v.tensor_scalar(qkv[:, t, :], src, wt, None, ALU.mult))
                    elif j == 0:
                        link(v.scalar_tensor_tensor(qkv[:, t, :], src, wt, qkv[:, t, :], ALU.mult, ALU.add))
                    else:
                        v.scalar_tensor_tensor(qkv[:, t, :], src, wt, qkv[:, t, :], ALU.mult, ALU.add)\
                         .then_inc(proj6_used, 1)
                        dve.wait_ge(proj6_used, k + 1)
            v.tensor_copy(small[:, 0:1], red[:, 0, 0:1]).then_inc(qkv_ready, 1)
            for t in range(TT):
                dve.wait_ge(score6, t + 1)
                lo = P if t % QT else 0
                if lo:
                    v.tensor_scalar(p6[:, t, 0:P], bank[:, 4 + t, 0:P], SCALE6, None, ALU.mult)
                link(v.scalar_tensor_tensor(p6[:, t, lo:lo + P], bank[:, 4 + t, lo:lo + P], SCALE6, causal[:, :],
                                            ALU.mult, ALU.add))
                v.tensor_reduce(row6[:, 2, t:t + 1], p6[:, t, 0:lo + P], AX.X, ALU.max, negate=True).then_inc(nmax6, 1)
            for t in range(TT):
                w = S if t % QT else P
                dve.wait_ge(exp6, t + 1)
                link(v.reciprocal(row6[:, 0, t:t + 1], row6[:, 3, t:t + 1]))
                v.tensor_scalar(p6[:, t, 0:w], p6[:, t, 0:w], row6[:, 0, t:t + 1], None, ALU.mult).then_inc(norm6, 1)
                dve.wait_ge(pT6_psum, t + 1)
                v.tensor_copy(pT6[:, t, :, :].rearrange("p a b -> p (a b)")[:, 0:w], bank[:, t % 2, 0:w])\
                 .then_inc(pT6_ready, 1)
            for t in range(TT):
                dve.wait_ge(att6, t + 1)
                if t >= 2:
                    dve.wait_ge(mixT_psum, t - 1)
                v.tensor_tensor(mixed[t % 2].rearrange("p (e d) -> p e d", d=HD6),
                                bank[:, 4 + t, 0:HD6].unsqueeze(1).broadcast_to([P, E6, HD6]),
                                weight[:, t, :].unsqueeze(2).broadcast_to([P, E6, HD6]), ALU.mult)\
                 .then_inc(mix_ready, 1)
            for t in range(TT):
                dve.wait_ge(y6_psum, t + 1)
                last = v.tensor_tensor(x[:, t, :], x[:, t, :], bank[:, 4 + t, 0:D], ALU.add)
            last.then_inc(x_final, 1)


def constants():
    n, f = np.arange(D)[:, None], np.arange(NF)[None, :]
    angle = 2 * np.pi * ((n * f) % D) / D
    share = np.where((f == 0) | (f == NF - 1), 1.0, 2.0) / D
    inverse = np.concatenate([(share * np.cos(angle)).T[:NF - 1], (-share * np.sin(angle)).T[:NF - 1],
                              (share * np.cos(angle)).T[NF - 1:]])
    i = np.arange(P)
    return {
        "c_ident": np.eye(P, dtype=np.float32),
        "c_tri": (i[:, None] <= i[None, :]).astype(np.float32),
        "c_causal": np.where(i[:, None] >= i[None, :], 0.0, -1e30).astype(np.float32),
        "c_rev": np.arange(16, 0, -1).astype(np.float32),
        "c_dft": np.concatenate([np.cos(angle), -np.sin(angle)], axis=1).astype(np.float32),
        "c_idft": inverse.astype(np.float32),
    }


def kernel(**inputs):
    import concourse.bacc as bacc
    from concourse.bass_utils import run_bass_kernel_spmd

    nc = bacc.Bacc("TRN2", target_bir_lowering=False, num_devices=1)
    arrays, views = {}, {}
    for name, value in list(inputs.items()) + list(constants().items()):
        array = np.ascontiguousarray(value)
        arrays[f"in_{name}"] = array
        views[name] = nc.dram_tensor(f"in_{name}", array.shape, mybir.dt.from_np(array.dtype),
                                     kind="ExternalInput").ap()
    out = nc.dram_tensor("out", (B, S, D), F32, kind="ExternalOutput").ap()
    build(nc, views, out)
    r = run_bass_kernel_spmd(nc, [arrays], core_ids=[0])
    return r.results[0]["out"]
```
